# Optimizing a Trainium2 kernel written in Bass

```python
import numpy as np
import jax
import jax.numpy as jnp

def _softmax(x, axis=-1):
    return jax.nn.softmax(x, axis=axis)

def _gelu(x):
    return jax.nn.gelu(x, approximate=True)

def _silu(x):
    return jax.nn.silu(x)

def _sigmoid(x):
    return jax.nn.sigmoid(x)

def _layernorm(x, axis=-1, eps=1e-05):
    m = jnp.mean(x, axis=axis, keepdims=True)
    v = jnp.var(x, axis=axis, keepdims=True)
    return (x - m) / jnp.sqrt(v + eps)

def _scatter_add(tgt, idx, src, axis=0):
    return tgt.at[idx].add(src)

def _segment_sum(src, seg, n):
    return jax.ops.segment_sum(src, seg, n)
kernel_name = 'mk_macaron_d1_jaxref_r4_055775'

def setup_inputs(seed: int=0):
    np.random.seed(seed)
    _w = jnp.asarray

    def _L0_attn_setup():
        import jax, jax.numpy as jnp
        import numpy as np
        D_MODEL = 256
        D_STATE = 16
        D_CONV = 4
        EXPAND = 2
        D_INNER = D_MODEL * EXPAND
        B_SZ = 2
        SEQ = 1024
        key = jax.random.key(seed)
        ks = jax.random.split(key, 11)
        rn = lambda i, shape, scale=1.0: jax.random.normal(ks[i], shape, jnp.float32) * scale
        return {'x': rn(0, (B_SZ, SEQ, D_MODEL)), 'W_in': rn(1, (D_MODEL, D_INNER), D_MODEL ** (-0.5)), 'b_in': rn(2, (D_INNER,), 0.01), 'conv_w': rn(3, (D_INNER, 1, D_CONV), 0.1), 'conv_b': rn(4, (D_INNER,), 0.01), 'A': rn(5, (D_STATE, D_STATE), 0.1), 'Bp': rn(6, (D_STATE,)), 'Cp': rn(7, (D_STATE,)), 'Dp': rn(8, (1,)), 'W_out': rn(9, (D_INNER, D_MODEL), D_INNER ** (-0.5)), 'b_out': rn(10, (D_MODEL,), 0.01)}
    _L0_attn_in = _L0_attn_setup()

    def _L0_ffn_setup():
        import jax, jax.numpy as jnp
        import numpy as np
        B, S, H, F, E = (1, 512, 256, 512, 8)

        def _swiglu(x, wg, wu, wd):
            return jax.nn.silu(x @ wg.T) * (x @ wu.T) @ wd.T
        key = jax.random.key(seed)
        ks = jax.random.split(key, 8)
        sc = 1.0 / np.sqrt(H)
        scf = 1.0 / np.sqrt(F)
        return {'hidden_states': jax.random.normal(ks[0], (B, S, H), jnp.float32), 'gate_w': jax.random.normal(ks[1], (E, H), jnp.float32) * sc, 'shared_gate': jax.random.normal(ks[2], (F, H), jnp.float32) * sc, 'shared_up': jax.random.normal(ks[3], (F, H), jnp.float32) * sc, 'shared_down': jax.random.normal(ks[4], (H, F), jnp.float32) * scf, 'r_gate': jax.random.normal(ks[5], (E, F, H), jnp.float32) * sc, 'r_up': jax.random.normal(ks[6], (E, F, H), jnp.float32) * sc, 'r_down': jax.random.normal(ks[7], (E, H, F), jnp.float32) * scf}
    _L0_ffn_in = _L0_ffn_setup()
    _d = {'L0_attn_x': _L0_attn_in['x'], 'L0_attn_W_in': _L0_attn_in['W_in'], 'L0_attn_b_in': _L0_attn_in['b_in'], 'L0_attn_conv_w': _L0_attn_in['conv_w'], 'L0_attn_conv_b': _L0_attn_in['conv_b'], 'L0_attn_A': _L0_attn_in['A'], 'L0_attn_Bp': _L0_attn_in['Bp'], 'L0_attn_Cp': _L0_attn_in['Cp'], 'L0_attn_Dp': _L0_attn_in['Dp'], 'L0_attn_W_out': _L0_attn_in['W_out'], 'L0_attn_b_out': _L0_attn_in['b_out'], 'L0_ffn_gate_w': _L0_ffn_in['gate_w'], 'L0_ffn_shared_gate': _L0_ffn_in['shared_gate'], 'L0_ffn_shared_up': _L0_ffn_in['shared_up'], 'L0_ffn_shared_down': _L0_ffn_in['shared_down'], 'L0_ffn_r_gate': _L0_ffn_in['r_gate'], 'L0_ffn_r_up': _L0_ffn_in['r_up'], 'L0_ffn_r_down': _L0_ffn_in['r_down']}
    _x0 = _d['L0_attn_x']
    _d['L0_attn_x'] = jax.random.normal(jax.random.fold_in(jax.random.key(seed), 1), (2, 2048, 256), dtype=_x0.dtype)
    del _x0
    return _d

def reference(L0_attn_x, L0_attn_W_in, L0_attn_b_in, L0_attn_conv_w, L0_attn_conv_b, L0_attn_A, L0_attn_Bp, L0_attn_Cp, L0_attn_Dp, L0_attn_W_out, L0_attn_b_out, L0_ffn_gate_w, L0_ffn_shared_gate, L0_ffn_shared_up, L0_ffn_shared_down, L0_ffn_r_gate, L0_ffn_r_up, L0_ffn_r_down):

    def _L0_attn_ref(x, W_in, b_in, conv_w, conv_b, A, Bp, Cp, Dp, W_out, b_out):
        import jax, jax.numpy as jnp
        import numpy as np
        D_MODEL = 256
        D_STATE = 16
        D_CONV = 4
        EXPAND = 2
        D_INNER = D_MODEL * EXPAND
        B_SZ = 2
        SEQ = 1024
        Bsz, S, _ = x.shape
        d_inner = W_in.shape[1]
        u = x @ W_in + b_in
        u = u.transpose(0, 2, 1)
        u = jax.lax.conv_general_dilated(u, conv_w, window_strides=(1,), padding=[(D_CONV - 1, 0)], dimension_numbers=('NCH', 'OIH', 'NCH'), feature_group_count=d_inner) + conv_b[None, :, None]
        u = u.transpose(0, 2, 1)
        At = jnp.tanh(A)

        def step(h, u_t):
            h = jnp.einsum('ij,bdj->bdi', At, h) + u_t[..., None] * Bp
            y = jnp.einsum('j,bdj->bd', Cp, h) + Dp[0] * u_t
            return (h, y)
        h0 = jnp.zeros((Bsz, d_inner, Bp.shape[0]), x.dtype)
        _, ys = jax.lax.scan(step, h0, u.transpose(1, 0, 2))
        y = jax.nn.silu(ys.transpose(1, 0, 2))
        return y @ W_out + b_out

    def _L0_ffn_ref(hidden_states, gate_w, shared_gate, shared_up, shared_down, r_gate, r_up, r_down):
        import jax, jax.numpy as jnp
        import numpy as np
        B, S, H, F, E = (1, 512, 256, 512, 8)

        def _swiglu(x, wg, wu, wd):
            return jax.nn.silu(x @ wg.T) * (x @ wu.T) @ wd.T
        b, s, h = hidden_states.shape
        x = hidden_states.reshape(-1, h)
        shared_out = _swiglu(x, shared_gate, shared_up, shared_down)
        logits = x @ gate_w.T
        top_id = jnp.argmax(logits, axis=-1)
        score = jax.nn.sigmoid(jnp.max(logits, axis=-1))
        xs = x * score[:, None]

        def body(acc, ws):
            wg, wu, wd, e = ws
            xe = jnp.where((top_id == e)[:, None], xs, 0.0)
            return (acc + _swiglu(xe, wg, wu, wd), None)
        acc0 = jnp.zeros_like(x)
        routed_out, _ = jax.lax.scan(body, acc0, (r_gate, r_up, r_down, jnp.arange(E)))
        return (shared_out + routed_out).reshape(b, s, h)
    x = L0_attn_x
    x = x + 0.5 * _L0_ffn_ref(_layernorm(x, axis=-1), L0_ffn_gate_w, L0_ffn_shared_gate, L0_ffn_shared_up, L0_ffn_shared_down, L0_ffn_r_gate, L0_ffn_r_up, L0_ffn_r_down)
    x = x + _L0_attn_ref(_layernorm(x, axis=-1), L0_attn_W_in, L0_attn_b_in, L0_attn_conv_w, L0_attn_conv_b, L0_attn_A, L0_attn_Bp, L0_attn_Cp, L0_attn_Dp, L0_attn_W_out, L0_attn_b_out)
    x = x + 0.5 * _L0_ffn_ref(_layernorm(x, axis=-1), L0_ffn_gate_w, L0_ffn_shared_gate, L0_ffn_shared_up, L0_ffn_shared_down, L0_ffn_r_gate, L0_ffn_r_up, L0_ffn_r_down)
    return x

_drawn_inputs = setup_inputs


def setup_inputs(seed=0):
    import zlib

    import numpy as np

    out = dict(_drawn_inputs(seed))
    spreads = {}
    factors = {'L0_attn_b_in': 5.005, 'L0_attn_b_out': 4.562}
    for name, (base, spread) in spreads.items():
        noise = np.random.default_rng([zlib.crc32(name.encode()), seed]).standard_normal(out[name].shape)
        drawn = base * np.exp(spread * noise) if base else spread * noise
        out[name] = jnp.asarray(drawn.astype(out[name].dtype))
    for name, factor in factors.items():
        out[name] = (out[name] * factor).astype(out[name].dtype)
    return out
```

```python
from contextlib import ExitStack

import concourse.bass as bass
from concourse import mybir

F32 = mybir.dt.float32
F32R = mybir.dt.float32r
BF16 = mybir.dt.bfloat16
I32 = mybir.dt.int32
ALU = mybir.AluOpType
ACT = mybir.ActivationFunctionType
AX = mybir.AxisListType

P = 128
LN_EPS = 1e-5


def build(nc, x, w_routed, w_shared, gate_w, w_in, w_out, vecs, b_out, ssm_a, ssm_bc, ssm_d, out):
    T, H = x.shape
    E, _, W = w_routed.shape
    C = w_in.shape[2]
    N = ssm_a.shape[0]
    KB = H // P
    FB = W // (2 * KB * P + H)
    F = FB * P
    CB = C // P
    GT = 4
    GN = GT * P
    NT = T // P
    NG = NT // GT
    NB = 2
    GB = NG // NB
    NS = NT + E - 1
    RING = 3
    assert NS % RING == 0 and W == 2 * KB * F + FB * H and GT == CB == FB
    UP0, DN0 = KB * F, 2 * KB * F
    ZN = P + N
    HB = CB * N

    xt = x.rearrange("(t p) h -> p t h", p=P)
    ot = out.rearrange("(t p) h -> p t h", p=P)
    xs_dram = nc.dram_tensor("xs_sorted", (NS * P, H), F32, kind="Internal").ap()
    ys_dram = nc.dram_tensor("ys_sorted", (NS * P, H), F32, kind="Internal").ap()
    xn_dram = nc.dram_tensor("xn_kept", (T, H), F32, kind="Internal").ap()
    xn = xn_dram.rearrange("(t p) h -> p t h", p=P)
    xs_slot = xs_dram.rearrange("(s p) h -> p s h", p=P)
    ys_slot = ys_dram.rearrange("(s p) h -> p s h", p=P)
    k_dram = nc.dram_tensor("k_padded", (1, 2 * P), F32, kind="Internal")
    oq_dram = nc.dram_tensor("obs_and_power", (N, ZN), F32, kind="Internal").ap()

    with ExitStack() as ctx:
        def sb(name, shape, dt, stack=ctx):
            return stack.enter_context(nc.sbuf_tensor(name, shape, dt))

        def sem(name):
            return ctx.enter_context(nc.semaphore(name))

        acc = sb("acc", [P, NT, H], F32)
        xg = sb("xg", [P, 2, GT, H], F32)
        ws_hi = sb("ws_hi", [P, W], F32R)
        ws_lo = sb("ws_lo", [P, W], F32R)
        rows = sb("rows", [P, 2 * GT, H], F32)
        xT_hi = sb("xT_hi", [P, KB, GN], F32R)
        xT_lo = sb("xT_lo", [P, KB, GN], F32R)
        sg = sb("sg", [P, 2, GN], F32)
        hf = sb("hf", [P, 2, GN], F32)
        xTf = sb("xTf", [P, KB, GN], F32)
        hT_hi = sb("hT_hi", [P, FB, GN], F32R)
        hT_lo = sb("hT_lo", [P, FB, GN], F32R)
        ident = sb("ident", [P, P], F32)
        anti = sb("anti", [P, P], F32)
        upper = sb("upper", [P, P], BF16)
        ones = sb("ones", [P, P], BF16)
        ones_r = sb("ones_r", [P, P], F32R)
        gw_f = sb("gw_f", [P, KB, E], F32)
        vec = sb("vec", [P, CB, 6], F32)
        tc_hi = sb("tc_hi", [P, ZN], F32R)
        tc_lo = sb("tc_lo", [P, ZN], F32R)
        rr_hi = sb("rr_hi", [P, 2, 2, ZN], F32R)
        rr_lo = sb("rr_lo", [P, 2, 2, ZN], F32R)
        bo_hl = sb("bo_hl", [P, H], F32R)
        stats = sb("stats", [P, 2, GT, 6], F32)
        mv = sb("mv", [P, 2, GT, 2], F32)
        ve = sb("ve", [P, 2, GT], F32)
        rstd = sb("rstd", [P, 2, GT], F32)
        mhalf = sb("mhalf", [P, GT], F32)
        lg = sb("lg", [P, NT, E], F32)
        mx = sb("mx", [P, NT], F32)
        score = sb("score", [P, NT], F32)
        pos = sb("pos", [P, NT], I32)
        slot_e = sb("slot_e", [1, NS], I32)
        after_e = sb("after_e", [1, E], I32)
        HH = sb("HH", [P, NB, P], F32R)

        shp = [P, NT, E]
        eq = sb("eq", shp, F32)
        oh = sb("oh", shp, BF16)
        pfx = sb("pfx", [P, 2, NT, E], F32)
        cum = sb("cum", [P, 2, NT, E], F32)
        pref = sb("pref", [P, 1, E], F32)
        thr = sb("thr", [P, 1, NT], F32)
        sidx = sb("sidx", [1, NS, 1], F32)
        cmp_t = sb("cmp_t", [P, E, NT], F32)
        m2 = sb("m2", [P, NT], F32)
        ne = sb("ne", [P, 4, E], F32)
        se = sb("se", [1, NS, E - 1], F32)
        sef = sb("sef", [1, NS], F32)

        routed = ExitStack()
        wr_raw = sb("wr_raw", [P, W], F32, routed)
        wr_hi = sb("wr_hi", [P, 2, W], F32R, routed)
        wr_lo = sb("wr_lo", [P, 2, W], F32R, routed)
        routed.close()
        over = ExitStack()
        wio_raw = sb("wio_raw", [P, 2, KB * C], F32, over)
        win_hi = sb("win_hi", [P, KB, C], F32R, over)
        win_lo = sb("win_lo", [P, KB, C], F32R, over)
        wout_hi = sb("wout_hi", [P, CB, H], F32R, over)
        wout_lo = sb("wout_lo", [P, CB, H], F32R, over)
        u = sb("u", [P, CB, 3 + GN], F32, over)
        halo = sb("halo", [P, NB, CB, 3], F32, over)
        v = sb("v", [P, 2, CB, GN], F32, over)
        vT_hi = sb("vT_hi", [P, C], F32R, over)
        vT_lo = sb("vT_lo", [P, C], F32R, over)
        yf = sb("yf", [P, 2, CB, P], F32, over)
        y_hi = sb("y_hi", [P, 2, CB, P], F32R, over)
        y_lo = sb("y_lo", [P, 2, CB, P], F32R, over)
        sf = sb("sf", [P, 2, CB, N], F32, over)
        over.close()
        setup = ExitStack()
        A2 = sb("A2", [N, 2 * N], F32, setup)
        bc = sb("bc", [N, 2], F32, setup)
        dd = sb("dd", [1, 1], F32, setup)
        PQ = sb("PQ", [N, 2, 2, N], F32, setup)
        At = sb("At", [N, N], F32, setup)
        VO = sb("VO", [N, 2, P], F32, setup)
        kpad = sb("kpad", [1, 2 * P], F32, setup)
        OQ = sb("OQ", [N, ZN], F32, setup)
        HV = sb("HV", [P, ZN], F32, setup)
        rf = sb("rf", [P, 2, 2, ZN], F32, setup)
        bo_f = sb("bo_f", [1, H], F32, setup)
        bo_t = sb("bo_t", [1, H], F32, setup)
        ws_raw = sb("ws_raw", [P, W], F32, setup)
        setup.close()
        def bank(name):
            return ctx.enter_context(nc.psum_tensor(name, [P, 512], F32))

        B = [bank(f"bank{i}") for i in range(8)]
        XT = B[0:2]
        LG = B[0]
        G2, U2, D2 = B[2:4], B[4:6], B[6:8]
        UB, VT, Z2, OB, SB_ = B[2], B[3], B[4:6], B[6], B[7]

        s_apart = sem("waited_apart")
        s_small = sem("small_loaded")
        s_x = [sem("x_loaded_even"), sem("x_loaded_odd")]
        s_wsraw = sem("ws_raw_loaded")
        s_const = sem("constants_made")
        s_setp = sem("setup_pe_done")
        s_setv = sem("setup_dve_done")
        s_seta = sem("setup_act_done")
        s_kst = sem("k_stored")
        s_hank = sem("hankel_loaded")
        s_oqst = sem("observation_stored")
        s_rf = sem("state_rows_loaded")
        s_wsh = sem("ws_hi_done")
        s_wsl = sem("ws_lo_done")
        s_zero = sem("xs_zeroed")
        s_st = sem("stats_done")
        s_mv = sem("mean_var_done")
        s_ve = sem("var_eps_done")
        s_rs = sem("rstd_done")
        s_xn = sem("xn_done")
        s_xc = [sem("xn_kept_even"), sem("xn_kept_odd")]
        s_xg = [sem("xg_loaded_even"), sem("xg_loaded_odd")]
        s_xt = sem("xT_transposed")
        s_xh = sem("xT_hi_done")
        s_xl = sem("xT_lo_done")
        s_xf = sem("xTf_done")
        s_lg = sem("logits_done")
        s_lgc = sem("logits_copied")
        s_rt = sem("route_steps")
        s_row = sem("row_steps")
        s_cum = sem("expert_rows_done")
        s_oh = sem("onehot_done")
        s_mx = sem("max_done")
        s_pf = sem("prefix_done")
        s_pfc = sem("prefix_copied")
        s_sc = sem("score_done")
        s_scl = sem("rows_scaled")
        s_rl = [sem("rows_loaded_even"), sem("rows_loaded_odd")]
        s_sct = [sem("scattered_even"), sem("scattered_odd")]
        s_tab = sem("slot_table_done")
        s_g = sem("gate_done")
        s_u = sem("up_done")
        s_sg = sem("silu_done")
        s_h = sem("h_done")
        s_hh = sem("h_hi_done")
        s_hl = sem("h_lo_done")
        s_d = sem("down_done")
        s_add = sem("shared_added")
        s_wraw = sem("wr_raw_loaded")
        s_wh = sem("wr_hi_done")
        s_wl = sem("wr_lo_done")
        s_slot = sem("slots_finished")
        s_xsl = [sem(f"xs_slot_loaded{j}") for j in range(RING)]
        s_mt = sem("m_xT_done")
        s_mxh = sem("m_xT_hi_done")
        s_mxl = sem("m_xT_lo_done")
        s_mg = sem("m_gate_done")
        s_mu = sem("m_up_done")
        s_msg = sem("m_silu_done")
        s_mh = sem("m_h_done")
        s_mth = sem("m_hT_done")
        s_mhh = sem("m_hT_hi_done")
        s_mhl = sem("m_hT_lo_done")
        s_ye = sem("m_y_copied")
        s_yst = [sem(f"y_stored{j}") for j in range(RING)]
        s_ga = [sem("gathered_even"), sem("gathered_odd")]
        s_fin = [sem(f"group_finished{g}") for g in range(NG)]
        s_out = sem("out_stored")
        s_wio = sem("w_io_loaded")
        s_wioh = sem("w_io_hi_done")
        s_wiol = sem("w_io_lo_done")
        s_ainit = sem("attn_zeroed")
        s_um = sem("u_done")
        s_ub = sem("u_in_sbuf")
        s_hal = sem("halo_placed")
        s_tap = sem("taps_done")
        s_v = sem("v_done")
        s_halo = sem("halo_saved")
        s_vt = sem("vT_transposed")
        s_vh = sem("vT_hi_done")
        s_vl = sem("vT_lo_done")
        s_z = sem("z_done")
        s_zs = sem("z_states_copied")
        s_stt = sem("states_transposed")
        s_sh = sem("states_hi_done")
        s_sl = sem("states_lo_done")
        s_y = sem("y_done")
        s_yh = sem("y_hi_done")
        s_yl = sem("y_lo_done")
        s_o = sem("w_out_done")
        s_x2 = sem("attn_added")

        block = ctx.enter_context(nc.Block())

        def f32(ap):
            return ap.bitcast(F32)

        def tiles(buf, g, n=GT):
            return buf[:, bass.ds(g * GT, n), :] if not isinstance(g, int) else buf[:, g * GT:g * GT + n, :]

        def wait_apart(eng, s, value):
            eng.wait_ge(s, value)
            eng.sem_inc(s_apart, 1)

        def t_r1(g): return g
        def t_s(L, g): return NG + g + L * 3 * NG
        def t_ln2(n): return 2 * NG + (n if isinstance(n, int) and n < 2 else 2 * n - 2)
        def t_ln3(n): return 2 * NG + (2 * n + 3 if not isinstance(n, int) or n < NG - 2 else n + NG)
        def c_s(L, g): return g + L * 2 * NG
        def c_ln2(n): return NG + n
        def f_r1(g): return g
        def f_ln3(n): return NG + n
        def k_r1(g): return g
        def k_ln2(n): return t_ln2(n) - NG
        def k_ln3(n): return t_ln3(n) - NG

        def mm3(pe, o, a_hi, a_lo, b_hi, b_lo, start, stop):
            pe.matmul(o, a_hi, b_hi, start=start, stop=False, skip_group_check=True)
            pe.matmul(o, a_lo, b_hi, start=False, stop=False, skip_group_check=True)
            return pe.matmul(o, a_hi, b_lo, start=False, stop=stop, skip_group_check=True)

        @block.tensor
        def _(pe):
            def setup_ssm():
                pe.wait_ge(s_seta, 1)
                m, step = 1, 0
                while m < P:
                    pe.wait_ge(s_setv, 3 + step)
                    Pm, Qm = PQ[:, step % 2, 0, :], PQ[:, step % 2, 1, :]
                    o = B[7]
                    kw = dict(skip_group_check=True)
                    pe.matmul(o[0:N, 0:m], Qm, VO[:, 0, 0:m], start=True, stop=True, **kw)
                    pe.matmul(o[0:N, P:P + m], Pm, VO[:, 1, 0:m], start=False, stop=True, **kw)
                    pe.matmul(o[0:N, 256:256 + N], Qm, Pm, start=False, stop=True, **kw)
                    pe.matmul(o[0:N, 256 + N:256 + 2 * N], Pm, Qm, start=False, stop=True,
                              **kw).then_inc(s_setp, 1)
                    m, step = 2 * m, step + 1
                pe.wait_ge(s_setv, 3 + step)
                pe.wait_ge(s_const, 6)
                pe.matmul(B[6][0:1, 0:P], bc[:, 1:2], VO[:, 0, :], start=True, stop=True,
                          skip_group_check=True)
                pe.matmul(B[6][0:N, P:2 * P], At[:, :], VO[:, 1, :], start=False, stop=True,
                          skip_group_check=True).then_inc(s_setp, 1)
                pe.transpose(B[5][:, 0:N], VO[:, 0, :], ident[0:N, 0:N]).then_inc(s_setp, 1)
                pe.wait_ge(s_hank, 16)
                pe.wait_ge(s_setv, 3 + step + 4)
                pe.matmul(B[5][:, 0:ZN], anti[:, :], HV[:, :], start=True, stop=True,
                          skip_group_check=True).then_inc(s_setp, 1)

            def transposes(place, ready_sem, ready, cuts, copies):
                pe.wait_ge(ready_sem, ready)
                if not isinstance(cuts, int) or cuts > 0:
                    pe.wait_ge(s_xl, 2 * cuts)
                if not isinstance(copies, int) or copies > 0:
                    pe.wait_ge(s_xf, 2 * copies)
                for kb in range(KB):
                    for t in range(GT):
                        mm = pe.transpose(XT[kb][:, t * P:(t + 1) * P],
                                          xg[:, place, t, kb * P:(kb + 1) * P], ident[:, :])
                    mm.then_inc(s_xt, 1)

            def logits(f):
                pe.wait_ge(s_xf, 2 * f + 2)
                for t in range(GT):
                    for kb in range(KB):
                        mm = pe.matmul(LG[:, t * E:(t + 1) * E], xTf[:, kb, t * P:(t + 1) * P], gw_f[:, kb, :],
                                       start=(t == 0 and kb == 0), stop=(kb == KB - 1), skip_group_check=True)
                mm.then_inc(s_lg, 1)

            def prefix(L):
                pe.wait_ge(s_oh, L + 1)
                o = G2[0]
                pe.matmul(o[:, 0:NT * E], upper[:, :], oh[:, :, :].rearrange("p t e -> p (t e)"),
                          start=True, stop=True, skip_group_check=True)
                pe.matmul(o[:, NT * E:2 * NT * E], ones[:, :], oh[:, :, :].rearrange("p t e -> p (t e)"),
                          start=False, stop=True, skip_group_check=True).then_inc(s_pf, 1)

            def shared_gu(L, g):
                n = L * NG + g
                pe.wait_ge(s_xl, 2 * c_s(L, g) + 2)
                for fb in range(FB):
                    if fb >= 2:
                        pe.wait_ge(s_h, 4 * n + fb - 1)
                    for o, c0, done in ((G2[fb % 2], 0, s_g), (U2[fb % 2], UP0, s_u)):
                        for kb in range(KB):
                            cs = slice(c0 + kb * F + fb * P, c0 + kb * F + (fb + 1) * P)
                            mm = mm3(pe, o[:, :], ws_hi[:, cs], ws_lo[:, cs], xT_hi[:, kb, :],
                                     xT_lo[:, kb, :], start=(kb == 0), stop=(kb == KB - 1))
                        mm.then_inc(done, 1)

            def shared_down(L, g):
                n = L * NG + g
                for fb in range(FB):
                    pe.wait_ge(s_hl, 4 * n + fb + 1)
                    for t in range(GT):
                        ts = slice(t * P, (t + 1) * P)
                        cs = slice(DN0 + fb * H, DN0 + (fb + 1) * H)
                        mm = mm3(pe, D2[t // 2][:, (t % 2) * H:(t % 2 + 1) * H], hT_hi[:, fb, ts],
                                 hT_lo[:, fb, ts], ws_hi[:, cs], ws_lo[:, cs],
                                 start=(fb == 0 and t % 2 == 0), stop=(fb == FB - 1))
                        if fb == FB - 1 and t % 2 == 1:
                            mm.then_inc(s_d, 1)

            def shared(L):
                uses = L * NG // 2
                pe.wait_ge(s_lgc, (L + 1) * NG)
                transposes(0, s_xg[0], 16 * (uses + 1), c_s(L, 0), (L + 1) * NG)
                shared_gu(L, 0)
                transposes(1, s_xg[1], 16 * (uses + 1), c_s(L, 1), 0)
                shared_down(L, 0)
                prefix(L)
                pe.wait_ge(s_pfc, L + 1)
                with pe.Fori(0, NG // 2 - 1) as h:
                    for a in (1, 2):
                        g = 2 * h + a
                        shared_gu(L, g)
                        transposes(1 - a % 2, s_xg[1 - a % 2], 16 * (h + (uses + 2)), c_s(L, g + 1), 0)
                        shared_down(L, g)
                shared_gu(L, NG - 1)
                shared_down(L, NG - 1)

            MXT, MG, MU, MHT, MY = B[0], B[2], B[3], B[4], B[6]

            def m_transpose(L, s, j, use):
                pe.wait_ge(s_xsl[j], 16 * (L * (NS // RING) + use + 1))
                for kb in range(KB):
                    mm = pe.transpose(MXT[:, kb * P:(kb + 1) * P], rows[:, j, kb * P:(kb + 1) * P],
                                      ident[:, :])
                mm.then_inc(s_mt, 1)

            def m_gate_up(L, s, e, par):
                q = L * NS + s
                pe.wait_ge(s_wl, e + (L * E + 1))
                pe.wait_ge(s_mxl, q + 1)
                for o, c0, done in ((MG, 0, s_mg), (MU, UP0, s_mu)):
                    for kb in range(KB):
                        cs = par * W + (c0 + kb * F)
                        wh = wr_hi[:, :, :].rearrange("p a w -> p (a w)")[:, bass.ds(cs, F)]
                        wl = wr_lo[:, :, :].rearrange("p a w -> p (a w)")[:, bass.ds(cs, F)]
                        mm = mm3(pe, o[:, :], xT_hi[:, kb, 0:P], xT_lo[:, kb, 0:P], wh, wl,
                                 start=(kb == 0), stop=(kb == KB - 1))
                    mm.then_inc(done, 1)

            def m_down(L, s, par):
                q = L * NS + s
                pe.wait_ge(s_mhl, q + 1)
                for fb in range(FB):
                    cs = par * W + (DN0 + fb * H)
                    wh = wr_hi[:, :, :].rearrange("p a w -> p (a w)")[:, bass.ds(cs, H)]
                    wl = wr_lo[:, :, :].rearrange("p a w -> p (a w)")[:, bass.ds(cs, H)]
                    mm = mm3(pe, MY[:, 0:H], hT_hi[:, fb, 0:P], hT_lo[:, fb, 0:P], wh, wl,
                             start=(fb == 0), stop=(fb == FB - 1))
                mm.then_inc(s_slot, 1)

            def m_transpose_h(L, s):
                pe.wait_ge(s_mh, L * NS + s + 1)
                for fb in range(FB):
                    mm = pe.transpose(MHT[:, fb * P:(fb + 1) * P], hf[:, 0, fb * P:(fb + 1) * P],
                                      ident[:, :])
                mm.then_inc(s_mth, 1)

            def expert_of(s):
                e = pe.value_load(slot_e[0:1, bass.ds(s, 1)], min_val=0, max_val=E - 1)
                return e, e % 2

            def routed_body(L, i, first=False, last=False):
                if not first:
                    prev = expert_of(i * RING - 1)[1]
                for j in range(RING):
                    s = i * RING + j
                    e, par = expert_of(s)
                    m_gate_up(L, s, e, par)
                    if not (last and j == RING - 1):
                        m_transpose(L, s + 1, (j + 1) % RING, i + (j + 1) // RING)
                    if not (first and j == 0):
                        m_down(L, s - 1, prev)
                    m_transpose_h(L, s)
                    prev = par
                if last:
                    m_down(L, i * RING + RING - 1, prev)

            def routed_slots(L):
                pe.wait_ge(s_tab, L + 1)
                pe.wait_ge(s_add, 2 * (L + 1) * NG)
                m_transpose(L, 0, 0, 0)
                routed_body(L, 0, first=True)
                with pe.Fori(1, NS // RING - 1) as i:
                    routed_body(L, i)
                routed_body(L, NS // RING - 1, last=True)

            def u_block(n, cb):
                if not (isinstance(n, int) and n == 0 and cb == 0):
                    pe.wait_ge(s_ub, 4 * n + cb)
                for kb in range(KB):
                    cs = slice(cb * P, (cb + 1) * P)
                    mm = mm3(pe, UB[:, :], win_hi[:, kb, cs], win_lo[:, kb, cs], xT_hi[:, kb, :],
                             xT_lo[:, kb, :], start=(kb == 0), stop=(kb == KB - 1))
                mm.then_inc(s_um, 1)

            def chunk(n, b, t):
                q = 4 * n + t
                first = isinstance(q, int) and q == 0
                if not first:
                    pe.wait_ge(s_y, q)
                pe.wait_ge(s_vl, q + 1)
                for cb in range(CB):
                    cs = slice(cb * P, (cb + 1) * P)
                    mm3(pe, Z2[cb // 2][:, (cb % 2) * ZN:(cb % 2 + 1) * ZN], vT_hi[:, cs], vT_lo[:, cs],
                        tc_hi[:, :], tc_lo[:, :], start=(cb % 2 == 0), stop=False)
                if not first:
                    pe.wait_ge(s_sl, q)
                for a in range(2):
                    zo = Z2[a][:, 0:2 * ZN]
                    pe.matmul(zo, HH[:, b, :], rr_hi[:, a, :, :].rearrange("p b z -> p (b z)"),
                              start=False, stop=False, skip_group_check=True)
                    mm = pe.matmul(zo, HH[:, b, :], rr_lo[:, a, :, :].rearrange("p b z -> p (b z)"),
                                   start=False, stop=True, skip_group_check=True)
                mm.then_inc(s_z, 1)

            def attn_group(n, b, prev=True, u_next=True, ln2_next=True):
                for t in range(GT):
                    q = 4 * n + t
                    if t == 0:
                        pe.wait_ge(s_v, 4 * n + 4)
                    if not (isinstance(q, int) and q == 0):
                        pe.wait_ge(s_vl, q)
                    for cb in range(CB):
                        mm = pe.transpose(VT[:, cb * P:(cb + 1) * P], v[:, b, cb, t * P:(t + 1) * P],
                                          ident[:, :])
                    mm.then_inc(s_vt, 1)
                    if u_next:
                        if t == 0:
                            pe.wait_ge(s_xl, 2 * c_ln2(n + 1) + 2)
                        u_block(n + 1, t)
                    chunk(n, b, t)
                    if t > 0:
                        w_out_part(n, t - 1)
                    elif prev:
                        w_out_part(n - 1, GT - 1)
                    pe.wait_ge(s_zs, q + 1)
                    pe.transpose(SB_[:, 0:P], sf[:, :, :, :].rearrange("p a c n -> p (a c n)"),
                                 ident[:, :]).then_inc(s_stt, 1)
                    if t == 2 and prev:
                        if isinstance(n, int) and n > 1:
                            pe.wait_ge(s_lgc, NG + n - 1)
                        transposes(1, s_xn, k_ln3(n - 1) + 1, c_ln2(n + 2) if ln2_next else c_ln2(NG), f_ln3(n - 1))
                        logits(f_ln3(n - 1))
                    if t == 3 and ln2_next:
                        if prev:
                            pe.wait_ge(s_lgc, NG + n)
                        transposes(0, s_xn, k_ln2(n + 2) + 1, c_ln2(n + 2), f_ln3(n) if prev else f_ln3(0))

            def w_out_part(n, t):
                pe.wait_ge(s_yl, 4 * n + t + 1)
                if t % 2 == 0 and not (isinstance(n, int) and n == t == 0):
                    pe.wait_ge(s_x2, 2 * n + t // 2)
                o = OB[:, (t % 2) * H:(t % 2 + 1) * H]
                pe.matmul(o, ones_r[:, :], bo_hl[:, :], start=(t % 2 == 0), stop=False,
                          skip_group_check=True)
                for cb in range(CB):
                    mm = mm3(pe, o, y_hi[:, t % 2, cb, :], y_lo[:, t % 2, cb, :], wout_hi[:, cb, :],
                             wout_lo[:, cb, :], start=False, stop=(cb == CB - 1))
                mm.then_inc(s_o, 1)

            def attention():
                transposes(0, s_xn, k_ln2(0) + 1, c_ln2(0), f_ln3(0))
                pe.wait_ge(s_xl, 2 * c_ln2(0) + 2)
                for cb in range(CB):
                    u_block(0, cb)
                transposes(0, s_xn, k_ln2(1) + 1, c_ln2(1), f_ln3(0))
                attn_group(0, 0, prev=False)
                attn_group(1, 1)
                with pe.Fori(1, GB - 1) as i:
                    for b in range(NB):
                        attn_group(NB * i + b, b)
                attn_group(NG - 2, 0, ln2_next=False)
                attn_group(NG - 1, 1, u_next=False, ln2_next=False)
                w_out_part(NG - 1, GT - 1)
                pe.wait_ge(s_lgc, 2 * NG - 1)
                transposes(1, s_xn, k_ln3(NG - 1) + 1, c_ln2(NG), f_ln3(NG - 1))
                logits(f_ln3(NG - 1))

            pe.sem_inc(s_slot, 1)
            setup_ssm()
            pe.wait_ge(s_const, 8)
            transposes(0, s_xn, 1, 0, 0)
            logits(0)
            pe.wait_ge(s_lgc, 1)
            transposes(1, s_xn, 2, 0, 1)
            logits(1)
            with pe.Fori(1, NG // 2) as h:
                for a in range(2):
                    m = 2 * h + a
                    pe.wait_ge(s_lgc, m)
                    transposes(a, s_xn, m + 1, 0, m)
                    logits(m)
            pe.wait_ge(s_wsl, 1)
            shared(0)
            routed_slots(0)
            pe.wait_ge(s_wiol, 2)
            attention()
            shared(1)
            routed_slots(1)

        @block.scalar
        def _(act):
            def hi(o, i):
                return act.activation(o, i, ACT.Copy)

            def xt_hi(m):
                for kb in range(KB):
                    act.wait_ge(s_xt, 2 * m + kb + 1)
                    hi(xT_hi[:, kb, :], XT[kb][:, :]).then_inc(s_xh, 1)

            def xt_copy(m):
                for kb in range(KB):
                    act.wait_ge(s_xt, 2 * m + kb + 1)
                    act.activation(xTf[:, kb, :], XT[kb][:, :], ACT.Copy).then_inc(s_xf, 1)

            def s_silu(L, g, fb):
                act.wait_ge(s_g, 4 * (L * NG + g) + fb + 1)
                act.activation(sg[:, fb % 2, :], G2[fb % 2][:, :], ACT.Silu).then_inc(s_sg, 1)

            def s_hi(L, g, fb):
                act.wait_ge(s_h, 4 * (L * NG + g) + fb + 1)
                hi(hT_hi[:, fb, :], hf[:, fb % 2, :]).then_inc(s_hh, 1)

            def shared_group(L, g, last=False):
                s_silu(L, g, 0)
                for fb in range(1, FB):
                    s_silu(L, g, fb)
                    s_hi(L, g, fb - 1)
                s_hi(L, g, FB - 1)
                if not last:
                    xt_hi(t_s(L, g + 1))

            def shared(L):
                xt_hi(t_s(L, 0))
                shared_group(L, 0)
                act.wait_ge(s_pf, L + 1)
                act.activation(pfx[:, :, :, :].rearrange("p a t e -> p (a t e)"), G2[0][:, :],
                               ACT.Copy).then_inc(s_pfc, 1)
                act.wait_ge(s_mx, L + 1)
                act.activation(score[:, :], mx[:, :], ACT.Sigmoid).then_inc(s_sc, 1)
                with act.Fori(1, NG - 1) as g:
                    shared_group(L, g)
                shared_group(L, NG - 1, last=True)

            MXT, MG, MHT, MY = B[0], B[2], B[4], B[6]

            def m_x_hi(L, s):
                act.wait_ge(s_mt, L * NS + s + 1)
                hi(xT_hi[:, :, 0:P], MXT[:, 0:KB * P].rearrange("p (k t) -> p k t", k=KB)).then_inc(s_mxh, 1)

            def m_y(L, s, j, use, fresh):
                act.wait_ge(s_slot, L * NS + s + 2)
                if not fresh:
                    act.wait_ge(s_yst[j], 16 * (L * (NS // RING) + use))
                act.activation(rows[:, GT + j, :], MY[:, 0:H], ACT.Copy, scale=0.5).then_inc(s_ye, 1)

            def routed_body(L, i, first=False, last=False):
                for j in range(RING):
                    s = i * RING + j
                    act.wait_ge(s_mg, L * NS + s + 1)
                    act.activation(sg[:, 0, :], MG[:, :], ACT.Silu).then_inc(s_msg, 1)
                    if not (last and j == RING - 1):
                        m_x_hi(L, s + 1)
                    if not (first and j == 0):
                        m_y(L, s - 1, (j - 1) % RING, i - (j == 0), L == 0 and first)
                    act.wait_ge(s_mth, L * NS + s + 1)
                    hi(hT_hi[:, :, 0:P], MHT[:, :].rearrange("p (f t) -> p f t", f=FB)).then_inc(s_mhh, 1)
                if last:
                    m_y(L, i * RING + RING - 1, RING - 1, i, False)

            def routed_slots(L):
                m_x_hi(L, 0)
                routed_body(L, 0, first=True)
                with act.Fori(1, NS // RING - 1) as i:
                    routed_body(L, i)
                routed_body(L, NS // RING - 1, last=True)

            def u_out(n, cb):
                act.wait_ge(s_um, 4 * n + cb + 1)
                if not (isinstance(n, int) and n == 0) and cb == 0:
                    act.wait_ge(s_halo, n)
                act.activation(u[:, cb, 3:3 + GN], UB[:, :], ACT.Identity,
                               bias=vec[:, cb, 5:6]).then_inc(s_ub, 1)

            def attn_group(n, b, prev=True, u_next=True, ln2_next=True):
                for t in range(GT):
                    q = 4 * n + t
                    act.wait_ge(s_vt, q + 1)
                    hi(vT_hi[:, :], VT[:, :]).then_inc(s_vh, 1)
                    if u_next:
                        u_out(n + 1, t)
                    act.wait_ge(s_zs, q + 1)
                    for a in range(2):
                        yact = act.activation(
                            yf[:, t % 2, 2 * a:2 * a + 2, :],
                            Z2[a][:, 0:2 * ZN].rearrange("p (c z) -> p c z", c=2)[:, :, 0:P], ACT.Silu)
                    yact.then_inc(s_y, 1)
                    act.wait_ge(s_y, q + 1)
                    hi(y_hi[:, t % 2, :, :], yf[:, t % 2, :, :]).then_inc(s_yh, 1)
                    act.wait_ge(s_stt, q + 1)
                    hi(HH[:, b, :], SB_[:, 0:P]).then_inc(s_sh, 1)
                    if t == 2 and prev:
                        xt_copy(t_ln3(n - 1))
                    if t == 3 and ln2_next:
                        xt_hi(t_ln2(n + 2))

            def attention():
                xt_hi(t_ln2(0))
                for cb in range(CB):
                    u_out(0, cb)
                xt_hi(t_ln2(1))
                attn_group(0, 0, prev=False)
                attn_group(1, 1)
                with act.Fori(1, GB - 1) as i:
                    for b in range(NB):
                        attn_group(NB * i + b, b)
                attn_group(NG - 2, 0, ln2_next=False)
                attn_group(NG - 1, 1, u_next=False, ln2_next=False)
                xt_copy(t_ln3(NG - 1))

            act.wait_ge(s_small, 16 * 6)
            act.activation(At[:, :], A2[:, 0:N], ACT.Tanh)
            act.activation(PQ[:, 0, :, :].rearrange("n a m -> n (a m)"), A2[:, :], ACT.Tanh).then_inc(s_seta, 1)
            act.wait_ge(s_setv, 15)
            hi(tc_hi[:, :], HV[:, :]).then_inc(s_seta, 1)
            act.wait_ge(s_rf, 16 * 2 * CB)
            hi(rr_hi[:, :, :, :], rf[:, :, :, :]).then_inc(s_seta, 1)
            act.wait_ge(s_wsraw, 16)
            hi(ws_hi[:, :], ws_raw[:, :]).then_inc(s_wsh, 1)
            with act.Fori(0, NG) as g:
                xt_copy(t_r1(g))
            shared(0)
            routed_slots(0)
            act.wait_ge(s_wio, 32)
            act.activation(win_hi[:, :, :].rearrange("p k c -> p (k c)"), wio_raw[:, 0, :],
                           ACT.Copy).then_inc(s_wioh, 1)
            act.activation(wout_hi[:, :, :].rearrange("p k c -> p (k c)"), wio_raw[:, 1, :],
                           ACT.Copy).then_inc(s_wioh, 1)
            act.wait_ge(s_ainit, 1)
            attention()
            shared(1)
            routed_slots(1)

        @block.vector
        def _(dve):
            def lo(o, full, h):
                return dve.tensor_tensor(o, full, f32(h), ALU.subtract)

            def xt_lo(c):
                for kb in range(KB):
                    dve.wait_ge(s_xh, 2 * c + kb + 1)
                    lo(xT_lo[:, kb, :], XT[kb][:, :], xT_hi[:, kb, :]).then_inc(s_xl, 1)

            def norm_stats(k, g, place):
                for t in range(GT):
                    ins = dve.bn_stats(stats[:, place, t, :], acc[:, bass.ds(g * GT + t, 1), :].squeeze(1))
                ins.then_inc(s_st, 1)
                wait_apart(dve, s_st, k + 1)
                for t in range(GT):
                    ins = dve.bn_aggr(mv[:, place, t, :], stats[:, place, t, :])
                ins.then_inc(s_mv, 1)

            def norm_apply(k, g, place, kept=None):
                dve.wait_ge(s_rs, k + 1)
                if kept is not None:
                    dve.wait_ge(s_xc[place], 16 * kept)
                for t in range(GT):
                    ts = bass.ds(g * GT + t, 1)
                    ins = dve.tensor_scalar(xg[:, place, t, :], acc[:, ts, :].squeeze(1),
                                            mv[:, place, t, 0:1], rstd[:, place, t:t + 1],
                                            ALU.subtract, ALU.mult)
                ins.then_inc(s_xn, 1)

            def copy_logits(g, count):
                dve.wait_ge(s_lg, count)
                dve.tensor_copy(tiles(lg, g), LG[:, 0:GT * E].rearrange("p (t e) -> p t e", t=GT)).then_inc(s_lgc, 1)

            steps = [0]

            def chained(ins):
                steps[0] += 1
                ins.then_inc(s_rt, 1)
                dve.wait_ge(s_rt, steps[0])

            def choose(L):
                def b3(ap):
                    return ap.unsqueeze(2).to_broadcast([P, NT, E])
                dve.wait_ge(s_lgc, (L + 1) * NG)
                dve.tensor_reduce(mx[:, :], lg[:, :, :], AX.X, ALU.max).then_inc(s_mx, 1)
                dve.wait_ge(s_mx, L + 1)
                chained(dve.tensor_tensor(eq[:, :, :], lg[:, :, :], b3(mx[:, :]), ALU.is_equal))
                chained(dve.tensor_tensor(eq[:, :, :], eq[:, :, :], pref[:, :, :].to_broadcast([P, NT, E]), ALU.mult))
                chained(dve.tensor_reduce(m2[:, :], eq[:, :, :], AX.X, ALU.max))
                dve.tensor_tensor(oh[:, :, :], eq[:, :, :], b3(m2[:, :]), ALU.is_equal).then_inc(s_oh, 1)

            def slot_tables(L):
                dve.wait_ge(s_pfc, L + 1)
                src, d, place = pfx[:, 1, :, :], 1, 0
                while d < NT:
                    dst = cum[:, place, :, :]
                    dve.tensor_copy(dst[:, 0:d, :], src[:, 0:d, :])
                    chained(dve.tensor_tensor(dst[:, d:NT, :], src[:, d:NT, :], src[:, 0:NT - d, :], ALU.add))
                    src, d, place = dst, 2 * d, 1 - place
                assert place == 1
                last = src[:, NT - 1:NT, :].rearrange("p a e -> p e a")
                chained(dve.tensor_tensor(cmp_t[:, :, :], last.to_broadcast([P, E, NT]),
                                       thr[:, :, :].to_broadcast([P, E, NT]), ALU.is_gt))
                chained(dve.tensor_reduce(ne[:, 3, :], cmp_t[:, :, :], AX.X, ALU.add))
                src, d, where = ne[:, 3, :], 1, 0
                while d < E:
                    dst = ne[:, where, :]
                    dve.tensor_copy(dst[:, 0:d], src[:, 0:d])
                    chained(dve.tensor_tensor(dst[:, d:E], src[:, d:E], src[:, 0:E - d], ALU.add))
                    src, d, where = dst, 2 * d, 1 - where
                before = ne[:, where, :]
                chained(dve.tensor_tensor(before, src, ne[:, 3, :], ALU.subtract))
                dve.tensor_scalar(ne[:, 2, :], before, float(P), None, ALU.mult).then_inc(s_cum, 1)
                dve.tensor_copy(after_e[:, :], src[0:1, :])
                chained(dve.tensor_tensor(se[:, :, :], sidx[:, :, :].to_broadcast([1, NS, E - 1]),
                                       src[0:1, 0:E - 1].unsqueeze(1).to_broadcast([1, NS, E - 1]), ALU.is_ge))
                chained(dve.tensor_reduce(sef[:, :], se[:, :, :], AX.X, ALU.add))
                dve.tensor_copy(slot_e[:, :], sef[:, :]).then_inc(s_tab, 1)

            def s_mult(L, g, fb):
                q = 4 * (L * NG + g) + fb
                dve.wait_ge(s_sg, q + 1)
                dve.wait_ge(s_u, q + 1)
                dve.tensor_tensor(hf[:, fb % 2, :], sg[:, fb % 2, :], U2[fb % 2][:, :],
                                  ALU.mult).then_inc(s_h, 1)

            def s_lo(L, g, fb):
                dve.wait_ge(s_hh, 4 * (L * NG + g) + fb + 1)
                lo(hT_lo[:, fb, :], hf[:, fb % 2, :], hT_hi[:, fb, :]).then_inc(s_hl, 1)

            def shared_group(L, g, last=False):
                n = L * NG + g
                s_mult(L, g, 0)
                for fb in range(1, FB):
                    if fb >= 2:
                        dve.wait_ge(s_hl, 4 * n + fb - 1)
                    s_mult(L, g, fb)
                    s_lo(L, g, fb - 1)
                s_lo(L, g, FB - 1)
                if not last:
                    xt_lo(c_s(L, g + 1))
                for a in range(2):
                    dve.wait_ge(s_d, 2 * n + a + 1)
                    half = acc[:, bass.ds(g * GT + 2 * a, 2), :]
                    dve.scalar_tensor_tensor(half, D2[a][:, :].rearrange("p (t h) -> p t h", t=2), 0.5, half,
                                             ALU.mult, ALU.add).then_inc(s_add, 1)

            def scale_rows(L, g, half, h):
                dve.wait_ge(s_rl[half], 16 * (h + (L * NG // 2 + 1)))
                for t in range(GT):
                    r = rows[:, half * GT + t, :]
                    ins = dve.tensor_scalar(r, r, score[:, bass.ds(g * GT + t, 1)], None, ALU.mult)
                ins.then_inc(s_scl, 1)

            def shared(L):
                choose(L)
                xt_lo(c_s(L, 0))
                shared_group(L, 0)
                slot_tables(L)
                dve.wait_ge(s_sc, L + 1)
                with dve.Fori(0, NG // 2 - 1) as h:
                    for a in (1, 2):
                        scale_rows(L, 2 * h + a - 1, a - 1, h)
                        shared_group(L, 2 * h + a)
                scale_rows(L, NG - 2, 0, NG // 2 - 1)
                scale_rows(L, NG - 1, 1, NG // 2 - 1)
                shared_group(L, NG - 1, last=True)

            MXT, MU, MHT = B[0], B[3], B[4]

            def m_x_lo(L, s):
                dve.wait_ge(s_mxh, L * NS + s + 1)
                lo(xT_lo[:, :, 0:P], MXT[:, 0:KB * P].rearrange("p (k t) -> p k t", k=KB),
                   xT_hi[:, :, 0:P]).then_inc(s_mxl, 1)

            def routed_body(L, i, last=False):
                for j in range(RING):
                    s = i * RING + j
                    dve.wait_ge(s_msg, L * NS + s + 1)
                    dve.wait_ge(s_mu, L * NS + s + 1)
                    dve.tensor_tensor(hf[:, 0, :], sg[:, 0, :], MU[:, :], ALU.mult).then_inc(s_mh, 1)
                    if not (last and j == RING - 1):
                        m_x_lo(L, s + 1)
                    dve.wait_ge(s_mhh, L * NS + s + 1)
                    lo(hT_lo[:, :, 0:P], MHT[:, :].rearrange("p (f t) -> p f t", f=FB),
                       hT_hi[:, :, 0:P]).then_inc(s_mhl, 1)

            def routed_slots(L):
                m_x_lo(L, 0)
                with dve.Fori(0, NS // RING - 1) as i:
                    routed_body(L, i)
                routed_body(L, NS // RING - 1, last=True)

            def conv_start(n, b):
                dve.tensor_copy(u[:, :, 0:3], halo[:, b, :, :]).then_inc(s_hal, 1)

            def tap(n, b, cb, k):
                q = 4 * n + cb
                vb = v[:, b, cb, :]
                if k == 3:
                    dve.wait_ge(s_hal, n + 1)
                    dve.wait_ge(s_ub, q + 1)
                    dve.tensor_scalar(vb, u[:, cb, 3:3 + GN], vec[:, cb, 3:4], vec[:, cb, 4:5],
                                      ALU.mult, ALU.add).then_inc(s_tap, 1)
                else:
                    dve.wait_ge(s_tap, 3 * q + 3 - k)
                    ins = dve.scalar_tensor_tensor(vb, u[:, cb, k:k + GN], vec[:, cb, k:k + 1], vb,
                                                   ALU.mult, ALU.add)
                    ins.then_inc(s_tap if k else s_v, 1)

            def save_halo(b):
                dve.tensor_copy(halo[:, b, :, :], u[:, :, GN:GN + 3]).then_inc(s_halo, 1)

            def attn_group(n, b, prev=True, u_next=True, ln2_next=True):
                g = group_of(n, b, 0)
                for t in range(GT):
                    q = 4 * n + t
                    if t == 0 and u_next:
                        conv_start(n + 1, 1 - b)
                    dve.wait_ge(s_vh, q + 1)
                    lo(vT_lo[:, :], VT[:, :], vT_hi[:, :]).then_inc(s_vl, 1)
                    if u_next:
                        tap(n + 1, 1 - b, t, 3)
                        tap(n + 1, 1 - b, t, 2)
                    dve.wait_ge(s_z, q + 1)
                    for a in range(2):
                        zin = Z2[a][:, 0:2 * ZN].rearrange("p (c z) -> p c z", c=2)[:, :, P:ZN]
                        dve.tensor_copy(sf[:, 0, 2 * a:2 * a + 2, :], zin)
                        ins = dve.tensor_copy(sf[:, 1, 2 * a:2 * a + 2, :], zin)
                    ins.then_inc(s_zs, 1)
                    if u_next:
                        tap(n + 1, 1 - b, t, 1)
                        tap(n + 1, 1 - b, t, 0)
                        if t == GT - 1:
                            save_halo(1 - b)
                    dve.wait_ge(s_sh, q + 1)
                    lo(HH[HB:2 * HB, b, :], SB_[HB:2 * HB, 0:P], HH[HB:2 * HB, b, :]).then_inc(s_sl, 1)
                    if t == 0 and prev:
                        add_out(n - 1, group_of(n, b, -1), 1)
                        wait_apart(dve, s_x2, 2 * n)
                        norm_stats(k_ln3(n - 1), group_of(n, b, -1), 1)
                    if t == 1 and prev:
                        norm_apply(k_ln3(n - 1), group_of(n, b, -1), 1, NG // 2 + n - 1)
                    if t == 2:
                        add_out(n, g, 0)
                        if ln2_next:
                            wait_apart(dve, s_ga[b], gathers_of(n, b, 2))
                            norm_stats(k_ln2(n + 2), group_of(n, b, 2), 0)
                    if t == 3:
                        if prev:
                            copy_logits(group_of(n, b, -1), NG + n)
                        if ln2_next:
                            norm_apply(k_ln2(n + 2), group_of(n, b, 2), 0)
                            xt_lo(c_ln2(n + 2))

            def attention():
                for n in range(2):
                    wait_apart(dve, s_ga[n], 64)
                    norm_stats(k_ln2(n), n * GB, 0)
                    norm_apply(k_ln2(n), n * GB, 0)
                    xt_lo(c_ln2(n))
                    if n == 0:
                        conv_start(0, 0)
                        for cb in range(CB):
                            for k in (3, 2, 1, 0):
                                tap(0, 0, cb, k)
                        save_halo(0)
                attn_group(0, 0, prev=False)
                attn_group(1, 1)
                with dve.Fori(1, GB - 1) as i:
                    for b in range(NB):
                        where[0] = i
                        attn_group(NB * i + b, b)
                where[0] = None
                attn_group(NG - 2, 0, ln2_next=False)
                attn_group(NG - 1, 1, u_next=False, ln2_next=False)
                last = (NB - 1) * GB + GB - 1
                add_out(NG - 1, last, 1)
                wait_apart(dve, s_x2, 2 * NG)
                norm_stats(k_ln3(NG - 1), last, 1)
                norm_apply(k_ln3(NG - 1), last, 1, NG // 2 + NG - 1)
                copy_logits(last, 2 * NG)

            where = [None]

            def group_of(n, b, d):
                i = where[0] if where[0] is not None else (n - b) // 2
                b2 = (b + d) % 2
                return b2 * GB + i + (b + d - b2) // 2

            def gathers_of(n, b, d):
                i = where[0] if where[0] is not None else (n - b) // 2
                return 64 * (i + (1 + d // 2))

            def add_out(n, g, a):
                dve.wait_ge(s_o, 4 * n + 2 * a + 2)
                half = acc[:, bass.ds(g * GT + 2 * a, 2), :]
                dve.tensor_tensor(half, half, OB[:, :].rearrange("p (t h) -> p t h", t=2),
                                  ALU.add).then_inc(s_x2, 1)

            dve.wait_ge(s_small, 16 * 6)
            dve.tensor_copy(VO[:, 0, 0:1], bc[:, 0:1]).then_inc(s_setv, 1)
            dve.tensor_copy(VO[:, 1, 0:1], bc[:, 1:2]).then_inc(s_setv, 1)
            dve.memset(kpad[:, :], 0.0).then_inc(s_setv, 1)
            m, step = 1, 0
            while m < P:
                dve.wait_ge(s_setp, step + 1)
                dve.tensor_copy(VO[:, :, m:2 * m],
                                B[7][0:N, 0:2 * P].rearrange("n (a m) -> n a m", a=2)[:, :, 0:m])
                dve.tensor_copy(PQ[:, (step + 1) % 2, :, :],
                                B[7][0:N, 256:256 + 2 * N].rearrange("n (a m) -> n a m", a=2)).then_inc(s_setv, 1)
                m, step = 2 * m, step + 1
            dve.wait_ge(s_seta, 1)
            dve.wait_ge(s_const, 8)
            dve.wait_ge(s_setp, 9)
            dve.tensor_copy(kpad[:, P - 1:2 * P - 1], B[6][0:1, 0:P]).then_inc(s_setv, 1)
            dve.wait_ge(s_setv, 11)
            dve.tensor_tensor(kpad[:, P - 1:P], kpad[:, P - 1:P], dd[:, :], ALU.add).then_inc(s_setv, 1)
            dve.tensor_copy(OQ[:, 0:P], B[6][0:N, P:2 * P])
            dve.wait_ge(s_setv, 10)
            dve.tensor_copy(OQ[:, P:ZN], PQ[:, 1, 1, :]).then_inc(s_setv, 1)
            dve.tensor_copy(HV[:, P:ZN], B[5][:, 0:N]).then_inc(s_setv, 1)
            dve.wait_ge(s_setp, 10)
            dve.tensor_copy(HV[:, :], B[5][:, 0:ZN]).then_inc(s_setv, 1)
            dve.wait_ge(s_seta, 2)
            dve.tensor_tensor(tc_lo[:, :], HV[:, :], f32(tc_hi[:, :]), ALU.subtract)
            dve.wait_ge(s_seta, 3)
            dve.tensor_tensor(rr_lo[0:HB, :, :, :].rearrange("p a b z -> p (a b z)"),
                              rf[0:HB, :, :, :].rearrange("p a b z -> p (a b z)"),
                              f32(rr_hi[0:HB, :, :, :].rearrange("p a b z -> p (a b z)")), ALU.subtract)
            dve.tensor_copy(bo_hl[0:1, :], bo_f[:, :]).then_inc(s_setv, 1)
            dve.wait_ge(s_setv, 16)
            dve.tensor_tensor(bo_t[:, :], bo_f[:, :], f32(bo_hl[0:1, :]), ALU.subtract).then_inc(s_setv, 1)
            dve.wait_ge(s_setv, 17)
            dve.tensor_copy(bo_hl[32:33, :], bo_t[:, :]).then_inc(s_setv, 1)
            dve.wait_ge(s_wsh, 1)
            dve.tensor_tensor(ws_lo[:, :], ws_raw[:, :], f32(ws_hi[:, :]), ALU.subtract).then_inc(s_wsl, 1)

            def first_stats(h, a):
                wait_apart(dve, s_x[a], 16 * (h + 1))
                norm_stats(k_r1(2 * h + a), 2 * h + a, a)

            def first_norms(h, last=False):
                for a in range(2):
                    m = 2 * h + a
                    if not (last and a == 1):
                        first_stats(h + a, 1 - a)
                    norm_apply(k_r1(m), m, a, None if isinstance(h, int) and h == 0 else h)
                    if not (isinstance(m, int) and m == 0):
                        copy_logits(m - 1, m)

            first_stats(0, 0)
            first_norms(0)
            with dve.Fori(1, NG // 2 - 1) as h:
                first_norms(h)
            first_norms(NG // 2 - 1, last=True)
            copy_logits(NG - 1, NG)
            shared(0)
            routed_slots(0)
            dve.wait_ge(s_wioh, 1)
            dve.tensor_tensor(win_lo[:, :, :].rearrange("p k c -> p (k c)"), wio_raw[:, 0, :],
                              f32(win_hi[:, :, :].rearrange("p k c -> p (k c)")), ALU.subtract).then_inc(s_wiol, 1)
            dve.wait_ge(s_wioh, 2)
            dve.tensor_tensor(wout_lo[:, :, :].rearrange("p k c -> p (k c)"), wio_raw[:, 1, :],
                              f32(wout_hi[:, :, :].rearrange("p k c -> p (k c)")), ALU.subtract).then_inc(s_wiol, 1)
            dve.memset(halo[:, :, :, :], 0.0)
            dve.memset(f32(HH[:, :, :]), 0.0).then_inc(s_ainit, 1)
            dve.wait_ge(s_ainit, 1)
            attention()
            shared(1)
            routed_slots(1)

        @block.gpsimd
        def _(pool):
            done = [0]

            def row_step(ins):
                done[0] += 1
                ins.then_inc(s_row, 1)
                pool.wait_ge(s_row, done[0])

            def rsqrt(k, place):
                wait_apart(pool, s_mv, k + 1)
                pool.tensor_scalar(ve[:, place, :], mv[:, place, :, 1:2].squeeze(2), LN_EPS, None,
                                   ALU.add).then_inc(s_ve, 1)
                pool.wait_ge(s_ve, k + 1)
                pool.tensor_tensor(rstd[:, place, :], ve[:, place, :], mhalf[:, :], ALU.pow).then_inc(s_rs, 1)

            def token_rows(L):
                pool.wait_ge(s_cum, L + 1)
                t3 = pfx[:, 0, :, :]
                row_step(pool.tensor_tensor(t3, t3, cum[:, 0, :, :], ALU.add))
                row_step(pool.tensor_tensor(t3, t3, pfx[:, 1, :, :], ALU.subtract))
                row_step(pool.tensor_tensor(t3, t3, ne[:, 2:3, :].to_broadcast([P, NT, E]), ALU.add))
                row_step(pool.tensor_tensor(t3, t3, oh[:, :, :], ALU.mult))
                d = E // 2
                while d >= 1:
                    row_step(pool.tensor_tensor(t3[:, :, 0:d], t3[:, :, 0:d], t3[:, :, d:2 * d], ALU.add))
                    d //= 2
                row_step(pool.tensor_copy(pos[:, :], t3[:, :, 0:1].squeeze(2)))

            def load_rows(L, g):
                n = L * NG + g
                if n >= 2:
                    pool.wait_ge(s_sct[g % 2], 64 * (n // 2))
                pool.dma_start(rows[:, g % 2 * GT:(g % 2 + 1) * GT, :], tiles(xn, g)).then_inc(s_rl[g % 2], 16)

            def scatter(L):
                for g in range(NG):
                    half, n = g % 2, L * NG + g
                    pool.wait_ge(s_scl, n + 1)
                    for t in range(GT):
                        tt = g * GT + t
                        pool.indirect_dma_start(
                            out=xs_dram, out_offset=bass.IndirectOffsetOnAxis(ap=pos[:, tt:tt + 1], axis=0),
                            in_=rows[:, half * GT + t, :], in_offset=None).then_inc(s_sct[half], 16)
                    if 1 <= g < NG - 1:
                        load_rows(L, g + 1)

            def load_expert(L, e, free=None):
                k = L * E + e
                if k > 0:
                    pool.wait_ge(s_wl, k)
                pool.dma_start(wr_raw[:, :], w_routed[e, :, :]).then_inc(s_wraw, 16)
                if free is not None:
                    wait_apart(pool, s_slot, free)
                pool.dma_start(wr_hi[:, e % 2, :], w_routed[e, :, :]).then_inc(s_wh, 16)

            def cut_expert(L, e):
                k = L * E + e
                pool.wait_ge(s_wraw, 16 * (k + 1))
                pool.wait_ge(s_wh, 16 * (k + 1))
                pool.tensor_tensor(wr_lo[:, e % 2, :], wr_raw[:, :], f32(wr_hi[:, e % 2, :]),
                                   ALU.subtract).then_inc(s_wl, 1)

            def first_experts(L):
                for e in range(2):
                    load_expert(L, e)
                    cut_expert(L, e)

            def experts(L):
                pool.wait_ge(s_tab, L + 1)
                for e in range(2, E):
                    end = pool.value_load(after_e[0:1, e - 2:e - 1], min_val=0, max_val=NS)
                    load_expert(L, e, end + (L * NS + 1))
                    cut_expert(L, e)

            def gather(g, s):
                for t in range(GT):
                    gather_tile(g, t, s)

            def gather_tile(g, t, s):
                tt = g * GT + t
                pool.indirect_dma_start(
                    out=acc[:, tt, :], out_offset=None, in_=ys_dram,
                    in_offset=bass.IndirectOffsetOnAxis(ap=pos[:, tt:tt + 1], axis=0),
                    compute_op=ALU.add).then_inc(s, 16)

            def y_all_stored(L):
                for j in range(RING):
                    pool.wait_ge(s_yst[j], 16 * (NS // RING) * (L + 1))

            def pstep(ins, n):
                ins.then_inc(s_const, 1)
                pool.wait_ge(s_const, n)

            pool.memset(ident[:, :], 0.0)
            pool.memset(anti[:, :], 0.0)
            pool.memset(mhalf[:, :], -0.5)
            pool.memset(f32(ones_r[:, :]), 1.0)
            pool.memset(upper[:, :], 0.0)
            pool.memset(f32(rr_lo[:, :, :, :]), 0.0)
            pool.memset(rf[:, :, :, :], 0.0)
            pool.memset(f32(bo_hl[:, :]), 0.0)
            pstep(pool.memset(ones[:, :], 1.0), 1)
            pstep(pool.affine_select(ident[:, :], ident[:, :], pattern=[[-1, P]], compare_op=ALU.not_equal,
                                     fill=1.0, base=0, channel_multiplier=1), 2)
            pstep(pool.affine_select(anti[:, :], anti[:, :], pattern=[[1, P]], compare_op=ALU.not_equal,
                                     fill=1.0, base=-(P - 1), channel_multiplier=1), 3)
            pstep(pool.affine_select(upper[:, :], upper[:, :], pattern=[[-1, P]], compare_op=ALU.is_ge,
                                     fill=1.0, base=0, channel_multiplier=1), 4)
            pstep(pool.iota(pref[:, :, :].rearrange("p a e -> p (a e)"), pattern=[[-1, E]], base=E,
                            channel_multiplier=0, allow_small_or_imprecise_dtypes=True), 5)
            pstep(pool.iota(thr[:, :, :].rearrange("p a e -> p (a e)"), pattern=[[P, NT]], base=0,
                            channel_multiplier=0, allow_small_or_imprecise_dtypes=True), 6)
            pstep(pool.iota(sidx[:, :, :].rearrange("p a e -> p (a e)"), pattern=[[1, NS]], base=0,
                            channel_multiplier=0, allow_small_or_imprecise_dtypes=True), 7)
            pool.memset(rows[:, :, :], 0.0).then_inc(s_const, 1)
            pool.wait_ge(s_const, 8)
            s0 = 0
            while s0 < NS:
                c = min(2 * GT, NS - s0)
                pool.dma_start(xs_slot[:, s0:s0 + c, :], rows[:, 0:c, :]).then_inc(s_zero, 16)
                s0 += c
            with pool.Fori(0, NG // 2) as h:
                for a in range(2):
                    rsqrt(k_r1(2 * h + a), a)
            pool.wait_ge(s_zero, 16 * ((NS + 2 * GT - 1) // (2 * GT)))
            pool.wait_ge(s_xc[0], 16 * (NG // 2))
            pool.wait_ge(s_xc[1], 16 * (NG // 2))
            for g in range(2):
                load_rows(0, g)
            pool.wait_ge(s_wsl, 1)
            first_experts(0)
            token_rows(0)
            scatter(0)
            experts(0)
            y_all_stored(0)
            gather(0, s_ga[0])
            gather(GB, s_ga[1])
            for n in range(2):
                rsqrt(k_ln2(n), 0)
            gather(1, s_ga[0])
            for n in range(NG):
                b, i = n % 2, n // 2
                for t in range(GT):
                    if t == 1 and n > 0:
                        rsqrt(k_ln3(n - 1), 1)
                    if t == 3 and n + 2 < NG:
                        rsqrt(k_ln2(n + 2), 0)
                    q = 4 * n + t
                    pool.wait_ge(s_yh, q + 1)
                    pool.tensor_tensor(y_lo[:, t % 2, :, :], yf[:, t % 2, :, :],
                                       f32(y_hi[:, t % 2, :, :]), ALU.subtract).then_inc(s_yl, 1)
                    if n + 3 < NG:
                        gather_tile((1 - b) * GB + (n + 3) // 2, t, s_ga[1 - b])
            rsqrt(k_ln3(NG - 1), 1)
            pool.wait_ge(s_xc[0], 16 * (NG // 2))
            pool.wait_ge(s_xc[1], 16 * (NG // 2 + NG))
            for g in range(2):
                load_rows(1, g)
            first_experts(1)
            token_rows(1)
            scatter(1)
            experts(1)
            y_all_stored(1)
            for g in range(NG):
                gather(g, s_fin[g])

        @block.sync
        def _(sp):
            sp.dma_start(A2[:, :], ssm_a).then_inc(s_small, 16)
            sp.dma_start(bc[:, :], ssm_bc).then_inc(s_small, 16)
            sp.dma_start(dd[:, :], ssm_d).then_inc(s_small, 16)
            sp.dma_start(gw_f[:, :, :], gate_w).then_inc(s_small, 16)
            sp.dma_start(vec[:, :, :], vecs).then_inc(s_small, 16)
            sp.dma_start(bo_f[:, :], b_out).then_inc(s_small, 16)
            for g in range(2):
                sp.dma_start(tiles(acc, g), tiles(xt, g)).then_inc(s_x[g], 16)
            sp.dma_start(ws_raw[:, :], w_shared).then_inc(s_wsraw, 16)
            for g in range(2, NG):
                sp.wait_ge(s_x[g % 2], 16 * (g // 2))
                sp.dma_start(tiles(acc, g), tiles(xt, g)).then_inc(s_x[g % 2], 16)
            sp.wait_ge(s_setv, 12)
            sp.dma_start(k_dram.ap(), kpad[:, :]).then_inc(s_kst, 16)
            sp.wait_ge(s_kst, 16)
            sp.wait_ge(s_setv, 14)
            hankel = bass.AP(k_dram, 0, [[1, P], [1, P]])
            sp.dma_start(HV[:, 0:P], hankel).then_inc(s_hank, 16)
            sp.dma_start(oq_dram, OQ[:, :]).then_inc(s_oqst, 16)
            sp.wait_ge(s_oqst, 16)
            sp.wait_ge(s_const, 1)
            for half in range(2):
                for cb in range(CB):
                    r0 = half * HB + cb * N
                    sp.dma_start(rf[r0:r0 + N, cb // 2, cb % 2, :], oq_dram).then_inc(s_rf, 16)

            def slot_load(L, s, j):
                sp.dma_start(rows[:, j, :], xs_slot[:, bass.ds(s, 1), :].squeeze(1)).then_inc(s_xsl[j], 16)

            def slot_store(L, s, j):
                sp.wait_ge(s_ye, L * NS + s + 1)
                sp.dma_start(ys_slot[:, bass.ds(s, 1), :].squeeze(1), rows[:, GT + j, :]).then_inc(s_yst[j], 16)

            def routed_slots(L):
                for a in range(2):
                    sp.wait_ge(s_sct[a], 64 * (NG // 2) * (L + 1))
                for j in range(RING):
                    slot_load(L, j, j)
                with sp.Fori(0, NS // RING - 1) as i:
                    for j in range(RING):
                        s = i * RING + j
                        sp.wait_ge(s_mt, L * NS + s + 1)
                        slot_load(L, s + RING, j)
                        slot_store(L, s, j)
                for j in range(RING):
                    slot_store(L, NS - RING + j, j)

            def keep(k, place, g):
                sp.wait_ge(s_xn, k + 1)
                sp.dma_start(tiles(xn, g), xg[:, place, :, :]).then_inc(s_xc[place], 16)

            def shared_loads(L):
                sp.wait_ge(s_xc[0], 16 * (NG // 2))
                sp.wait_ge(s_xc[1], 16 * (NG // 2 + L * NG))
                with sp.Fori(0, NG // 2) as h:
                    for a in range(2):
                        g = 2 * h + a
                        sp.wait_ge(s_xt, 2 * (t_s(L, g) - 1))
                        sp.dma_start(xg[:, a, :, :], tiles(xn, g)).then_inc(s_xg[a], 16)

            with sp.Fori(0, NG // 2) as h:
                for a in range(2):
                    keep(k_r1(2 * h + a), a, 2 * h + a)
            shared_loads(0)
            routed_slots(0)
            sp.wait_ge(s_slot, NS + 1)
            sp.dma_start(wio_raw[:, 0, :], w_in.rearrange("p k c -> p (k c)")).then_inc(s_wio, 16)
            sp.dma_start(wio_raw[:, 1, :], w_out.rearrange("p k c -> p (k c)")).then_inc(s_wio, 16)
            with sp.Fori(0, GB - 1) as i:
                for b in range(NB):
                    keep(k_ln3(NB * i + b), 1, b * GB + i)
            for b in range(NB):
                keep(k_ln3(NG - NB + b), 1, b * GB + GB - 1)
            shared_loads(1)
            routed_slots(1)
            for g in range(NG):
                sp.wait_ge(s_fin[g], 16 * GT)
                sp.dma_start(tiles(ot, g), tiles(acc, g)).then_inc(s_out, 16)
            sp.wait_ge(s_out, 16 * NG)


def kernel(L0_attn_x, L0_attn_W_in, L0_attn_b_in, L0_attn_conv_w, L0_attn_conv_b, L0_attn_A, L0_attn_Bp,
           L0_attn_Cp, L0_attn_Dp, L0_attn_W_out, L0_attn_b_out, L0_ffn_gate_w, L0_ffn_shared_gate,
           L0_ffn_shared_up, L0_ffn_shared_down, L0_ffn_r_gate, L0_ffn_r_up, L0_ffn_r_down):
    import numpy as np
    import concourse.bacc as bacc
    from concourse.bass_utils import run_bass_kernel_spmd

    x = np.asarray(L0_attn_x)
    nb, s, h = x.shape

    def blocks(w):
        return np.ascontiguousarray(w.reshape(-1, P, w.shape[-1]).transpose(1, 0, 2))

    def expert(g, u, d):
        return np.concatenate([blocks(np.asarray(w).T).reshape(P, -1) for w in (g, u, d)], axis=1)

    r_g, r_u, r_d = (np.asarray(w) for w in (L0_ffn_r_gate, L0_ffn_r_up, L0_ffn_r_down))
    A = np.asarray(L0_attn_A)
    cw = np.asarray(L0_attn_conv_w)[:, 0, :]
    per_channel = np.concatenate([cw, np.asarray(L0_attn_conv_b)[:, None], np.asarray(L0_attn_b_in)[:, None]], axis=1)
    arrays = {
        "x": x.reshape(nb * s, h),
        "w_routed": np.stack([expert(r_g[e], r_u[e], r_d[e]) for e in range(r_g.shape[0])]),
        "w_shared": expert(L0_ffn_shared_gate, L0_ffn_shared_up, L0_ffn_shared_down),
        "gate_w": blocks(np.asarray(L0_ffn_gate_w).T),
        "w_in": blocks(np.asarray(L0_attn_W_in)),
        "w_out": blocks(np.asarray(L0_attn_W_out)),
        "vecs": blocks(per_channel),
        "b_out": np.asarray(L0_attn_b_out)[None, :],
        "ssm_a": np.concatenate([A, A.T], axis=1),
        "ssm_bc": np.stack([np.asarray(L0_attn_Bp), np.asarray(L0_attn_Cp)], axis=1),
        "ssm_d": np.asarray(L0_attn_Dp)[None, :],
    }
    arrays = {k: np.ascontiguousarray(a) for k, a in arrays.items()}
    nc = bacc.Bacc("TRN2", target_bir_lowering=False, num_devices=1)
    aps = {k: nc.dram_tensor(k, a.shape, mybir.dt.from_np(a.dtype), kind="ExternalInput").ap()
           for k, a in arrays.items()}
    out = nc.dram_tensor("out", (nb * s, h), F32, kind="ExternalOutput").ap()
    build(nc, *aps.values(), out)
    r = run_bass_kernel_spmd(nc, [arrays], core_ids=[0])
    return r.results[0]["out"].reshape(nb, s, h)
```

```python
from contextlib import ExitStack

import concourse.bass as bass
from concourse import mybir

F32 = mybir.dt.float32
F32R = mybir.dt.float32r
BF16 = mybir.dt.bfloat16
I32 = mybir.dt.int32
ALU = mybir.AluOpType
ACT = mybir.ActivationFunctionType
AX = mybir.AxisListType

P = 128
LN_EPS = 1e-5


def build(nc, x, w_routed, w_shared, gate_w, w_in, w_out, vecs, b_out, ssm_a, ssm_bc, ssm_d, out):
    T, H = x.shape
    E, _, W = w_routed.shape
    C = w_in.shape[2]
    N = ssm_a.shape[0]
    KB = H // P
    FB = W // (2 * KB * P + H)
    F = FB * P
    CB = C // P
    GT = 4
    GN = GT * P
    NT = T // P
    NG = NT // GT
    NB = 2
    GB = NG // NB
    NH = NG // 2
    NS = NT + E - 1
    RING = 3
    assert NS % RING == 0 and W == 2 * KB * F + FB * H and GT == CB == FB
    UP0, DN0 = KB * F, 2 * KB * F
    ZERO_STORES = -(-NS // (2 * GT))
    ZN = P + N
    HB = CB * N

    xt = x.rearrange("(t p) h -> p t h", p=P)
    ot = out.rearrange("(t p) h -> p t h", p=P)
    xs_dram = nc.dram_tensor("xs_sorted", (NS * P, H), F32, kind="Internal").ap()
    ys_dram = nc.dram_tensor("ys_sorted", (NS * P, H), F32, kind="Internal").ap()
    xn_dram = nc.dram_tensor("xn_kept", (T, H), F32, kind="Internal").ap()
    xn = xn_dram.rearrange("(t p) h -> p t h", p=P)
    xs_slot = xs_dram.rearrange("(s p) h -> p s h", p=P)
    ys_slot = ys_dram.rearrange("(s p) h -> p s h", p=P)
    k_dram = nc.dram_tensor("k_padded", (1, 2 * P), F32, kind="Internal")
    oq_dram = nc.dram_tensor("obs_and_power", (N, ZN), F32, kind="Internal").ap()

    with ExitStack() as ctx:
        def sb(name, shape, dt, stack=ctx):
            return stack.enter_context(nc.sbuf_tensor(name, shape, dt))

        def sem(name):
            return ctx.enter_context(nc.semaphore(name))

        acc = sb("acc", [P, NT, H], F32)
        xg = sb("xg", [P, 2, GT, H], F32)
        ws_hi = sb("ws_hi", [P, W], F32R)
        ws_lo = sb("ws_lo", [P, W], F32R)
        rows = sb("rows", [P, 2 * GT, H], F32)
        xT_hi = sb("xT_hi", [P, KB, GN], F32R)
        xT_lo = sb("xT_lo", [P, KB, GN], F32R)
        sg = sb("sg", [P, 2, GN], F32)
        hf = sb("hf", [P, 2, GN], F32)
        xTf = sb("xTf", [P, KB, GN], F32)
        hT_hi = sb("hT_hi", [P, FB, GN], F32R)
        hT_lo = sb("hT_lo", [P, FB, GN], F32R)
        ident = sb("ident", [P, P], F32)
        anti = sb("anti", [P, P], F32)
        upper = sb("upper", [P, P], BF16)
        ones = sb("ones", [P, P], BF16)
        ones_r = sb("ones_r", [P, P], F32R)
        gw_f = sb("gw_f", [P, KB, E], F32)
        vec = sb("vec", [P, CB, 6], F32)
        tc_hi = sb("tc_hi", [P, ZN], F32R)
        tc_lo = sb("tc_lo", [P, ZN], F32R)
        rr_hi = sb("rr_hi", [P, 2, 2, ZN], F32R)
        rr_lo = sb("rr_lo", [P, 2, 2, ZN], F32R)
        bo_hl = sb("bo_hl", [P, H], F32R)
        stats = sb("stats", [P, 2, GT, 6], F32)
        mv = sb("mv", [P, 2, GT, 2], F32)
        ve = sb("ve", [P, 2, GT], F32)
        rstd = sb("rstd", [P, 2, GT], F32)
        mhalf = sb("mhalf", [P, GT], F32)
        lg = sb("lg", [P, NT, E], F32)
        mx = sb("mx", [P, NT], F32)
        score = sb("score", [P, NT], F32)
        pos = sb("pos", [P, NT], I32)
        slot_e = sb("slot_e", [1, NS], I32)
        after_e = sb("after_e", [1, E], I32)
        HH = sb("HH", [P, NB, P], F32R)

        shp = [P, NT, E]
        eq = sb("eq", shp, F32)
        oh = sb("oh", shp, BF16)
        pfx = sb("pfx", [P, 2, NT, E], F32)
        cum = sb("cum", [P, 2, NT, E], F32)
        pref = sb("pref", [P, 1, E], F32)
        thr = sb("thr", [P, 1, NT], F32)
        sidx = sb("sidx", [1, NS, 1], F32)
        cmp_t = sb("cmp_t", [P, E, NT], F32)
        m2 = sb("m2", [P, NT], F32)
        ne = sb("ne", [P, 4, E], F32)
        se = sb("se", [1, NS, E - 1], F32)
        sef = sb("sef", [1, NS], F32)

        routed = ExitStack()
        wr_raw = sb("wr_raw", [P, W], F32, routed)
        wr_hi = sb("wr_hi", [P, 2, W], F32R, routed)
        wr_lo = sb("wr_lo", [P, 2, W], F32R, routed)
        routed.close()
        over = ExitStack()
        wio_raw = sb("wio_raw", [P, 2, KB * C], F32, over)
        win_hi = sb("win_hi", [P, KB, C], F32R, over)
        win_lo = sb("win_lo", [P, KB, C], F32R, over)
        wout_hi = sb("wout_hi", [P, CB, H], F32R, over)
        wout_lo = sb("wout_lo", [P, CB, H], F32R, over)
        u = sb("u", [P, CB, 3 + GN], F32, over)
        halo = sb("halo", [P, NB, CB, 3], F32, over)
        v = sb("v", [P, 2, CB, GN], F32, over)
        vT_hi = sb("vT_hi", [P, C], F32R, over)
        vT_lo = sb("vT_lo", [P, C], F32R, over)
        yf = sb("yf", [P, 2, CB, P], F32, over)
        y_hi = sb("y_hi", [P, 2, CB, P], F32R, over)
        y_lo = sb("y_lo", [P, 2, CB, P], F32R, over)
        sf = sb("sf", [P, 2, CB, N], F32, over)
        over.close()
        setup = ExitStack()
        A2 = sb("A2", [N, 2 * N], F32, setup)
        bc = sb("bc", [N, 2], F32, setup)
        dd = sb("dd", [1, 1], F32, setup)
        PQ = sb("PQ", [N, 2, 2, N], F32, setup)
        At = sb("At", [N, N], F32, setup)
        VO = sb("VO", [N, 2, P], F32, setup)
        kpad = sb("kpad", [1, 2 * P], F32, setup)
        OQ = sb("OQ", [N, ZN], F32, setup)
        HV = sb("HV", [P, ZN], F32, setup)
        rf = sb("rf", [P, 2, 2, ZN], F32, setup)
        bo_f = sb("bo_f", [1, H], F32, setup)
        bo_t = sb("bo_t", [1, H], F32, setup)
        ws_raw = sb("ws_raw", [P, W], F32, setup)
        setup.close()
        def bank(name):
            return ctx.enter_context(nc.psum_tensor(name, [P, 512], F32))

        B = [bank(f"bank{i}") for i in range(8)]
        XT = B[0:2]
        LG = B[0]
        LG1, XT1, xTf1 = B[3], (B[0:2], (B[2], B[4])), (xTf, hf)
        G2, U2, D2 = B[2:4], B[4:6], B[6:8]
        UB, VT, Z2, OB, SB_ = B[2], B[3], B[4:6], B[6], B[7]

        s_apart = sem("waited_apart")
        s_small = sem("small_loaded")
        s_x = [sem(f"x_loaded{g}") for g in range(NG)]
        s_wsraw = sem("ws_raw_loaded")
        s_const = sem("constants_made")
        s_setp = sem("setup_pe_done")
        s_setv = sem("setup_dve_done")
        s_seta = sem("setup_act_done")
        s_kst = sem("k_stored")
        s_hank = sem("hankel_loaded")
        s_oqst = sem("observation_stored")
        s_rf = sem("state_rows_loaded")
        s_wsh = sem("ws_hi_done")
        s_wsl = sem("ws_lo_done")
        s_zero = sem("xs_zeroed")
        s_st = sem("stats_done")
        s_mv = sem("mean_var_done")
        s_ve = sem("var_eps_done")
        s_rs = sem("rstd_done")
        s_xn = sem("xn_done")
        s_xc = [sem("xn_kept_even"), sem("xn_kept_odd")]
        s_xg = [sem("xg_loaded_even"), sem("xg_loaded_odd")]
        s_xt = sem("xT_transposed")
        s_xh = sem("xT_hi_done")
        s_xl = sem("xT_lo_done")
        s_xf = sem("xTf_done")
        s_lg = sem("logits_done")
        s_lgc = sem("logits_copied")
        s_rt = sem("route_steps")
        s_row = sem("row_steps")
        s_cum = sem("expert_rows_done")
        s_oh = sem("onehot_done")
        s_mx = sem("max_done")
        s_pf = sem("prefix_done")
        s_pfc = sem("prefix_copied")
        s_sc = sem("score_done")
        s_scl = sem("rows_scaled")
        s_rl = [sem("rows_loaded_even"), sem("rows_loaded_odd")]
        s_sct = [sem("scattered_even"), sem("scattered_odd")]
        s_tab = sem("slot_table_done")
        s_g = sem("gate_done")
        s_u = sem("up_done")
        s_sg = sem("silu_done")
        s_h = sem("h_done")
        s_hh = sem("h_hi_done")
        s_hl = sem("h_lo_done")
        s_d = sem("down_done")
        s_add = sem("shared_added")
        s_wraw = sem("wr_raw_loaded")
        s_wh = sem("wr_hi_done")
        s_wl = sem("wr_lo_done")
        s_slot = sem("slots_finished")
        s_xsl = [sem(f"xs_slot_loaded{j}") for j in range(RING)]
        s_mt = sem("m_xT_done")
        s_mxh = sem("m_xT_hi_done")
        s_mxl = sem("m_xT_lo_done")
        s_mg = sem("m_gate_done")
        s_mu = sem("m_up_done")
        s_msg = sem("m_silu_done")
        s_mh = sem("m_h_done")
        s_mth = sem("m_hT_done")
        s_mhh = sem("m_hT_hi_done")
        s_mhl = sem("m_hT_lo_done")
        s_ye = sem("m_y_copied")
        s_yst = [sem(f"y_stored{j}") for j in range(RING)]
        s_ga = [sem("gathered_even"), sem("gathered_odd")]
        s_fin = [sem(f"last_gathered{g}") for g in range(NG)]
        s_out = sem("out_stored")
        s_wio = sem("w_io_loaded")
        s_wioh = sem("w_io_hi_done")
        s_wiol = sem("w_io_lo_done")
        s_ainit = sem("attn_zeroed")
        s_um = sem("u_done")
        s_ub = sem("u_in_sbuf")
        s_hal = sem("halo_placed")
        s_tap3 = sem("last_tap_done")
        s_tap = sem("taps_done")
        s_v = sem("v_done")
        s_halo = sem("halo_saved")
        s_vt = sem("vT_transposed")
        s_vh = sem("vT_hi_done")
        s_vl = sem("vT_lo_done")
        s_z = sem("z_done")
        s_zs = sem("z_states_copied")
        s_stt = sem("states_transposed")
        s_sh = sem("states_hi_done")
        s_sl = sem("states_lo_done")
        s_y = sem("y_done")
        s_yh = sem("y_hi_done")
        s_yl = sem("y_lo_done")
        s_o = sem("w_out_done")
        s_x2 = sem("attn_added")

        block = ctx.enter_context(nc.Block())

        def f32(ap):
            return ap.bitcast(F32)

        def tiles(buf, g, n=GT):
            return buf[:, bass.ds(g * GT, n), :] if not isinstance(g, int) else buf[:, g * GT:g * GT + n, :]

        def wait_apart(eng, s, value):
            eng.wait_ge(s, value)
            eng.sem_inc(s_apart, 1)

        def half_groups(half): return range(half * NH, (half + 1) * NH)

        def t_r1(g): return g
        def t_s(L, g): return NG + g + L * 3 * NG
        def t_ln2(n): return 2 * NG + (n if isinstance(n, int) and n < 2 else 2 * n - 2)
        def t_ln3(n): return 2 * NG + (2 * n + 3 if not isinstance(n, int) or n < NG - 2 else n + NG)
        def c_s(L, g): return g + L * 2 * NG
        def c_ln2(n): return NG + n
        def f_r1(g): return g
        def f_ln3(n): return NG + n
        def k_r1(g): return g
        def k_ln2(n): return t_ln2(n) - NG
        def k_ln3(n): return t_ln3(n) - NG

        def mm3(pe, o, a_hi, a_lo, b_hi, b_lo, start, stop):
            pe.matmul(o, a_hi, b_hi, start=start, stop=False, skip_group_check=True)
            pe.matmul(o, a_lo, b_hi, start=False, stop=False, skip_group_check=True)
            return pe.matmul(o, a_hi, b_lo, start=False, stop=stop, skip_group_check=True)

        @block.tensor
        def _(pe):
            def setup_ssm():
                pe.wait_ge(s_seta, 1)
                m, step = 1, 0
                while m < P:
                    pe.wait_ge(s_setv, 3 + step)
                    Pm, Qm = PQ[:, step % 2, 0, :], PQ[:, step % 2, 1, :]
                    o = B[7]
                    kw = dict(skip_group_check=True)
                    pe.matmul(o[0:N, 0:m], Qm, VO[:, 0, 0:m], start=True, stop=True, **kw)
                    pe.matmul(o[0:N, P:P + m], Pm, VO[:, 1, 0:m], start=False, stop=True, **kw)
                    pe.matmul(o[0:N, 256:256 + N], Qm, Pm, start=False, stop=True, **kw)
                    pe.matmul(o[0:N, 256 + N:256 + 2 * N], Pm, Qm, start=False, stop=True,
                              **kw).then_inc(s_setp, 1)
                    m, step = 2 * m, step + 1

            def setup_response():
                pe.wait_ge(s_setv, 10)
                pe.matmul(B[6][0:1, 0:P], bc[:, 1:2], VO[:, 0, :], start=True, stop=True,
                          skip_group_check=True)
                pe.matmul(B[6][0:N, P:2 * P], At[:, :], VO[:, 1, :], start=False, stop=True,
                          skip_group_check=True).then_inc(s_setp, 1)
                pe.transpose(B[5][:, 0:N], VO[:, 0, :], ident[0:N, 0:N]).then_inc(s_setp, 1)

            def setup_toeplitz():
                pe.wait_ge(s_hank, 16)
                pe.wait_ge(s_setv, 14)
                pe.matmul(B[5][:, 0:ZN], anti[:, :], HV[:, :], start=True, stop=True,
                          skip_group_check=True).then_inc(s_setp, 1)

            def transposes(place, ready_sem, ready, cuts, copies, banks=XT):
                pe.wait_ge(ready_sem, ready)
                if not isinstance(cuts, int) or cuts > 0:
                    pe.wait_ge(s_xl, 2 * cuts)
                if not isinstance(copies, int) or copies > 0:
                    pe.wait_ge(s_xf, 2 * copies)
                for kb in range(KB):
                    for t in range(GT):
                        mm = pe.transpose(banks[kb][:, t * P:(t + 1) * P],
                                          xg[:, place, t, kb * P:(kb + 1) * P], ident[:, :])
                    mm.then_inc(s_xt, 1)

            def logits(f, bank=LG, src=xTf):
                pe.wait_ge(s_xf, 2 * f + 2)
                for t in range(GT):
                    for kb in range(KB):
                        mm = pe.matmul(bank[:, t * E:(t + 1) * E], src[:, kb, t * P:(t + 1) * P], gw_f[:, kb, :],
                                       start=(t == 0 and kb == 0), stop=(kb == KB - 1), skip_group_check=True)
                mm.then_inc(s_lg, 1)

            def prefix(L):
                pe.wait_ge(s_oh, L + 1)
                o = D2[0]
                pe.matmul(o[:, 0:NT * E], upper[:, :], oh[:, :, :].rearrange("p t e -> p (t e)"),
                          start=True, stop=True, skip_group_check=True)
                pe.matmul(o[:, NT * E:2 * NT * E], ones[:, :], oh[:, :, :].rearrange("p t e -> p (t e)"),
                          start=False, stop=True, skip_group_check=True).then_inc(s_pf, 1)

            def shared_gu(L, g):
                n = L * NG + g
                pe.wait_ge(s_xl, 2 * c_s(L, g) + 2)
                for fb in range(FB):
                    if fb >= 2:
                        pe.wait_ge(s_h, 4 * n + fb - 1)
                    for o, c0, done in ((G2[fb % 2], 0, s_g), (U2[fb % 2], UP0, s_u)):
                        for kb in range(KB):
                            cs = slice(c0 + kb * F + fb * P, c0 + kb * F + (fb + 1) * P)
                            mm = mm3(pe, o[:, :], ws_hi[:, cs], ws_lo[:, cs], xT_hi[:, kb, :],
                                     xT_lo[:, kb, :], start=(kb == 0), stop=(kb == KB - 1))
                        mm.then_inc(done, 1)

            def shared_down(L, g):
                n = L * NG + g
                for fb in range(FB):
                    pe.wait_ge(s_hl, 4 * n + fb + 1)
                    for t in range(GT):
                        ts = slice(t * P, (t + 1) * P)
                        cs = slice(DN0 + fb * H, DN0 + (fb + 1) * H)
                        mm = mm3(pe, D2[t // 2][:, (t % 2) * H:(t % 2 + 1) * H], hT_hi[:, fb, ts],
                                 hT_lo[:, fb, ts], ws_hi[:, cs], ws_lo[:, cs],
                                 start=(fb == 0 and t % 2 == 0), stop=(fb == FB - 1))
                        if fb == FB - 1 and t % 2 == 1:
                            mm.then_inc(s_d, 1)

            def shared(L, half):
                for g in half_groups(half):
                    if g == half * NH:
                        if half == 0:
                            pe.wait_ge(s_lgc, (L + 1) * NG)
                        shared_transposes(L, g)
                    if g == 0:
                        prefix(L)
                    shared_gu(L, g)
                    if g + 1 < (half + 1) * NH:
                        shared_transposes(L, g + 1)
                    elif L == 0 and half == 1:
                        transposes(0, s_xn, k_ln2(0) + 1, c_ln2(0), f_ln3(0))
                    if g == NH:
                        pe.wait_ge(s_ye, (L + 1) * NS)
                    if g == 0:
                        pe.wait_ge(s_pfc, L + 1)
                    shared_down(L, g)

            def shared_transposes(L, g):
                transposes(g % 2, s_xg[g % 2], 16 * (L * NH + g // 2 + 1), c_s(L, g), (L + 1) * NG)

            MXT, MG, MU, MHT, MY = B[0], B[2], B[3], B[4], B[6]

            def m_transpose(L, s, j, use):
                pe.wait_ge(s_xsl[j], 16 * (L * (NS // RING) + use + 1))
                for kb in range(KB):
                    mm = pe.transpose(MXT[:, kb * P:(kb + 1) * P], rows[:, j, kb * P:(kb + 1) * P],
                                      ident[:, :])
                mm.then_inc(s_mt, 1)

            def m_gate_up(L, s, e, par):
                q = L * NS + s
                pe.wait_ge(s_wl, e + (L * E + 1))
                pe.wait_ge(s_mxl, q + 1)
                for o, c0, done in ((MG, 0, s_mg), (MU, UP0, s_mu)):
                    for kb in range(KB):
                        cs = par * W + (c0 + kb * F)
                        wh = wr_hi[:, :, :].rearrange("p a w -> p (a w)")[:, bass.ds(cs, F)]
                        wl = wr_lo[:, :, :].rearrange("p a w -> p (a w)")[:, bass.ds(cs, F)]
                        mm = mm3(pe, o[:, :], xT_hi[:, kb, 0:P], xT_lo[:, kb, 0:P], wh, wl,
                                 start=(kb == 0), stop=(kb == KB - 1))
                    mm.then_inc(done, 1)

            def m_down(L, s, par):
                q = L * NS + s
                pe.wait_ge(s_mhl, q + 1)
                for fb in range(FB):
                    cs = par * W + (DN0 + fb * H)
                    wh = wr_hi[:, :, :].rearrange("p a w -> p (a w)")[:, bass.ds(cs, H)]
                    wl = wr_lo[:, :, :].rearrange("p a w -> p (a w)")[:, bass.ds(cs, H)]
                    mm = mm3(pe, MY[:, 0:H], hT_hi[:, fb, 0:P], hT_lo[:, fb, 0:P], wh, wl,
                             start=(fb == 0), stop=(fb == FB - 1))
                mm.then_inc(s_slot, 1)

            def m_transpose_h(L, s):
                pe.wait_ge(s_mh, L * NS + s + 1)
                for fb in range(FB):
                    mm = pe.transpose(MHT[:, fb * P:(fb + 1) * P], hf[:, 0, fb * P:(fb + 1) * P],
                                      ident[:, :])
                mm.then_inc(s_mth, 1)

            def expert_of(s):
                e = pe.value_load(slot_e[0:1, bass.ds(s, 1)], min_val=0, max_val=E - 1)
                return e, e % 2

            def routed_body(L, i, first=False, last=False):
                if not first:
                    prev = expert_of(i * RING - 1)[1]
                for j in range(RING):
                    s = i * RING + j
                    e, par = expert_of(s)
                    m_gate_up(L, s, e, par)
                    if not (last and j == RING - 1):
                        m_transpose(L, s + 1, (j + 1) % RING, i + (j + 1) // RING)
                    if not (first and j == 0):
                        m_down(L, s - 1, prev)
                    m_transpose_h(L, s)
                    prev = par
                if last:
                    m_down(L, i * RING + RING - 1, prev)

            def routed_slots(L):
                pe.wait_ge(s_tab, L + 1)
                pe.wait_ge(s_add, 2 * (L * NG + NH))
                m_transpose(L, 0, 0, 0)
                routed_body(L, 0, first=True)
                rounds, each = NS // RING - 2, 3
                with pe.Fori(0, rounds // each) as h:
                    for a in range(each):
                        routed_body(L, each * h + (a + 1))
                for i in range(rounds // each * each, rounds):
                    routed_body(L, i + 1)
                routed_body(L, NS // RING - 1, last=True)

            def u_block(n, cb):
                if not (isinstance(n, int) and n == 0 and cb == 0):
                    pe.wait_ge(s_ub, 4 * n + cb)
                for kb in range(KB):
                    cs = slice(cb * P, (cb + 1) * P)
                    mm = mm3(pe, UB[:, :], win_hi[:, kb, cs], win_lo[:, kb, cs], xT_hi[:, kb, :],
                             xT_lo[:, kb, :], start=(kb == 0), stop=(kb == KB - 1))
                mm.then_inc(s_um, 1)

            def chunk(n, b, t):
                q = 4 * n + t
                first = isinstance(q, int) and q == 0
                if not first:
                    pe.wait_ge(s_y, q)
                pe.wait_ge(s_vl, q + 1)
                for cb in range(CB):
                    cs = slice(cb * P, (cb + 1) * P)
                    mm3(pe, Z2[cb // 2][:, (cb % 2) * ZN:(cb % 2 + 1) * ZN], vT_hi[:, cs], vT_lo[:, cs],
                        tc_hi[:, :], tc_lo[:, :], start=(cb % 2 == 0), stop=False)
                if not first:
                    pe.wait_ge(s_sl, q)
                for a in range(2):
                    zo = Z2[a][:, 0:2 * ZN]
                    pe.matmul(zo, HH[:, b, :], rr_hi[:, a, :, :].rearrange("p b z -> p (b z)"),
                              start=False, stop=False, skip_group_check=True)
                    mm = pe.matmul(zo, HH[:, b, :], rr_lo[:, a, :, :].rearrange("p b z -> p (b z)"),
                                   start=False, stop=True, skip_group_check=True)
                mm.then_inc(s_z, 1)

            def attn_group(n, b, prev=True, u_next=True, ln2_next=True):
                for t in range(GT):
                    q = 4 * n + t
                    if t == 0:
                        pe.wait_ge(s_v, 4 * n + 4)
                    if not (isinstance(q, int) and q == 0):
                        pe.wait_ge(s_vl, q)
                    for cb in range(CB):
                        mm = pe.transpose(VT[:, cb * P:(cb + 1) * P], v[:, b, cb, t * P:(t + 1) * P],
                                          ident[:, :])
                    mm.then_inc(s_vt, 1)
                    if u_next:
                        if t == 0:
                            pe.wait_ge(s_xl, 2 * c_ln2(n + 1) + 2)
                        u_block(n + 1, t)
                    if t == 2 and prev:
                        if isinstance(n, int) and n > 1:
                            pe.wait_ge(s_lgc, NG + n - 1)
                        transposes(1, s_xn, k_ln3(n - 1) + 1, c_ln2(n + 2) if ln2_next else c_ln2(NG), f_ln3(n - 1))
                    if t == 3 and ln2_next:
                        if prev:
                            pe.wait_ge(s_lgc, NG + n)
                        transposes(0, s_xn, k_ln2(n + 2) + 1, c_ln2(n + 2), f_ln3(n) if prev else f_ln3(0))
                    chunk(n, b, t)
                    if t > 0:
                        w_out_part(n, t - 1)
                    elif prev:
                        w_out_part(n - 1, GT - 1)
                    pe.wait_ge(s_zs, q + 1)
                    pe.transpose(SB_[:, 0:P], sf[:, :, :, :].rearrange("p a c n -> p (a c n)"),
                                 ident[:, :]).then_inc(s_stt, 1)
                    if t == 2 and prev:
                        logits(f_ln3(n - 1))

            def w_out_part(n, t):
                pe.wait_ge(s_yl, 4 * n + t + 1)
                if t % 2 == 0 and not (isinstance(n, int) and n == t == 0):
                    pe.wait_ge(s_x2, 2 * n + t // 2)
                o = OB[:, (t % 2) * H:(t % 2 + 1) * H]
                pe.matmul(o, ones_r[:, :], bo_hl[:, :], start=(t % 2 == 0), stop=False,
                          skip_group_check=True)
                for cb in range(CB):
                    mm = mm3(pe, o, y_hi[:, t % 2, cb, :], y_lo[:, t % 2, cb, :], wout_hi[:, cb, :],
                             wout_lo[:, cb, :], start=False, stop=(cb == CB - 1))
                mm.then_inc(s_o, 1)

            def attention():
                pe.wait_ge(s_wiol, 2)
                pe.wait_ge(s_xl, 2 * c_ln2(0) + 2)
                for cb in range(CB):
                    u_block(0, cb)
                transposes(0, s_xn, k_ln2(1) + 1, c_ln2(1), f_ln3(0))
                pe.wait_ge(s_add, 2 * NG)
                attn_group(0, 0, prev=False)
                attn_group(1, 1)
                with pe.Fori(1, GB - 1) as i:
                    for b in range(NB):
                        attn_group(NB * i + b, b)
                attn_group(NG - 2, 0, ln2_next=False)
                attn_group(NG - 1, 1, u_next=False, ln2_next=False)
                w_out_part(NG - 1, GT - 1)
                pe.wait_ge(s_lgc, 2 * NG - 1)
                transposes(1, s_xn, k_ln3(NG - 1) + 1, c_ln2(NG), f_ln3(NG - 1))
                logits(f_ln3(NG - 1))

            pe.sem_inc(s_slot, 1)
            setup_ssm()
            pe.wait_ge(s_const, 3)
            transposes(0, s_xn, 1, 0, 0, XT1[0])
            for g in range(NG):
                if g + 1 < NG:
                    transposes((g + 1) % 2, s_xn, g + 2, 0, f_r1(g), XT1[(g + 1) % 2])
                if g > 0:
                    pe.wait_ge(s_lgc, g)
                logits(f_r1(g), LG1, xTf1[g % 2])
                if g == 0:
                    setup_response()
                if g == 4:
                    setup_toeplitz()
            pe.wait_ge(s_wsl, 1)
            shared(0, 0)
            routed_slots(0)
            shared(0, 1)
            attention()
            shared(1, 0)
            routed_slots(1)
            shared(1, 1)

        @block.scalar
        def _(act):
            def hi(o, i):
                return act.activation(o, i, ACT.Copy)

            def xt_hi(m):
                for kb in range(KB):
                    act.wait_ge(s_xt, 2 * m + kb + 1)
                    hi(xT_hi[:, kb, :], XT[kb][:, :]).then_inc(s_xh, 1)

            def xt_copy(m, dst=xTf, banks=XT):
                for kb in range(KB):
                    act.wait_ge(s_xt, 2 * m + kb + 1)
                    act.activation(dst[:, kb, :], banks[kb][:, :], ACT.Copy).then_inc(s_xf, 1)

            def s_silu(L, g, fb):
                act.wait_ge(s_g, 4 * (L * NG + g) + fb + 1)
                act.activation(sg[:, fb % 2, :], G2[fb % 2][:, :], ACT.Silu).then_inc(s_sg, 1)

            def s_hi(L, g, fb):
                act.wait_ge(s_h, 4 * (L * NG + g) + fb + 1)
                hi(hT_hi[:, fb, :], hf[:, fb % 2, :]).then_inc(s_hh, 1)

            def shared_group(L, g, following):
                s_silu(L, g, 0)
                for fb in range(1, FB):
                    s_silu(L, g, fb)
                    s_hi(L, g, fb - 1)
                s_hi(L, g, FB - 1)
                if following is not None:
                    xt_hi(following)

            def shared(L, half):
                xt_hi(t_s(L, half * NH))
                if half == 0:
                    act.wait_ge(s_pf, L + 1)
                    act.activation(pfx[:, :, :, :].rearrange("p a t e -> p (a t e)"), D2[0][:, :],
                                   ACT.Copy).then_inc(s_pfc, 1)
                    act.wait_ge(s_mx, L + 1)
                    act.activation(score[:, :], mx[:, :], ACT.Sigmoid).then_inc(s_sc, 1)
                for g in half_groups(half):
                    shared_group(L, g, t_s(L, g + 1) if g % NH < NH - 1 else t_ln2(0) if L == 0 and half else None)
                    if L == 0 and g == NH:
                        cut_w_io()

            MXT, MG, MHT, MY = B[0], B[2], B[4], B[6]

            def m_x_hi(L, s):
                act.wait_ge(s_mt, L * NS + s + 1)
                hi(xT_hi[:, :, 0:P], MXT[:, 0:KB * P].rearrange("p (k t) -> p k t", k=KB)).then_inc(s_mxh, 1)

            def m_y(L, s, j, use, fresh):
                act.wait_ge(s_slot, L * NS + s + 2)
                if not fresh:
                    act.wait_ge(s_yst[j], 16 * (L * (NS // RING) + use))
                act.activation(rows[:, GT + j, :], MY[:, 0:H], ACT.Copy, scale=0.5).then_inc(s_ye, 1)

            def routed_body(L, i, first=False, last=False):
                for j in range(RING):
                    s = i * RING + j
                    act.wait_ge(s_mg, L * NS + s + 1)
                    act.activation(sg[:, 0, :], MG[:, :], ACT.Silu).then_inc(s_msg, 1)
                    if not (last and j == RING - 1):
                        m_x_hi(L, s + 1)
                    if not (first and j == 0):
                        m_y(L, s - 1, (j - 1) % RING, i - (j == 0), L == 0 and first)
                    act.wait_ge(s_mth, L * NS + s + 1)
                    hi(hT_hi[:, :, 0:P], MHT[:, :].rearrange("p (f t) -> p f t", f=FB)).then_inc(s_mhh, 1)
                if last:
                    m_y(L, i * RING + RING - 1, RING - 1, i, False)

            def routed_slots(L):
                m_x_hi(L, 0)
                routed_body(L, 0, first=True)
                with act.Fori(1, NS // RING - 1) as i:
                    routed_body(L, i)
                routed_body(L, NS // RING - 1, last=True)

            def u_out(n, cb):
                act.wait_ge(s_um, 4 * n + cb + 1)
                if not (isinstance(n, int) and n == 0) and cb == 0:
                    act.wait_ge(s_halo, n)
                act.activation(u[:, cb, 3:3 + GN], UB[:, :], ACT.Identity,
                               bias=vec[:, cb, 5:6]).then_inc(s_ub, 1)

            def last_tap(n, b, cb):
                act.wait_ge(s_ub, 4 * n + cb + 1)
                act.activation(v[:, b, cb, :], u[:, cb, 3:3 + GN], ACT.Identity, bias=vec[:, cb, 4:5],
                               scale=vec[:, cb, 3:4]).then_inc(s_tap3, 1)

            def attn_group(n, b, prev=True, u_next=True, ln2_next=True):
                for t in range(GT):
                    q = 4 * n + t
                    act.wait_ge(s_vt, q + 1)
                    hi(vT_hi[:, :], VT[:, :]).then_inc(s_vh, 1)
                    if u_next:
                        u_out(n + 1, t)
                        last_tap(n + 1, 1 - b, t)
                    if t == 2 and prev:
                        xt_copy(t_ln3(n - 1))
                    if t == 3 and ln2_next:
                        xt_hi(t_ln2(n + 2))
                    act.wait_ge(s_zs, q + 1)
                    for a in range(2):
                        yact = act.activation(
                            yf[:, t % 2, 2 * a:2 * a + 2, :],
                            Z2[a][:, 0:2 * ZN].rearrange("p (c z) -> p c z", c=2)[:, :, 0:P], ACT.Silu)
                    yact.then_inc(s_y, 1)
                    act.wait_ge(s_y, q + 1)
                    hi(y_hi[:, t % 2, :, :], yf[:, t % 2, :, :]).then_inc(s_yh, 1)
                    act.wait_ge(s_stt, q + 1)
                    hi(HH[:, b, :], SB_[:, 0:P]).then_inc(s_sh, 1)

            def attention():
                for cb in range(CB):
                    u_out(0, cb)
                    last_tap(0, 0, cb)
                xt_hi(t_ln2(1))
                attn_group(0, 0, prev=False)
                attn_group(1, 1)
                with act.Fori(1, GB - 1) as i:
                    for b in range(NB):
                        attn_group(NB * i + b, b)
                attn_group(NG - 2, 0, ln2_next=False)
                attn_group(NG - 1, 1, u_next=False, ln2_next=False)
                xt_copy(t_ln3(NG - 1))

            def cut_w_io():
                act.wait_ge(s_wio, 32)
                act.activation(win_hi[:, :, :].rearrange("p k c -> p (k c)"), wio_raw[:, 0, :],
                               ACT.Copy).then_inc(s_wioh, 1)
                act.activation(wout_hi[:, :, :].rearrange("p k c -> p (k c)"), wio_raw[:, 1, :],
                               ACT.Copy).then_inc(s_wioh, 1)

            act.wait_ge(s_small, 16 * 6)
            act.activation(At[:, :], A2[:, 0:N], ACT.Tanh)
            act.activation(PQ[:, 0, :, :].rearrange("n a m -> n (a m)"), A2[:, :], ACT.Tanh).then_inc(s_seta, 1)
            for g in range(NG):
                xt_copy(t_r1(g), xTf1[g % 2], XT1[g % 2])
                if g == 4:
                    act.wait_ge(s_rf, 16 * 2 * CB)
                    hi(rr_hi[:, :, :, :], rf[:, :, :, :]).then_inc(s_seta, 1)
                if g == 5:
                    act.wait_ge(s_wsraw, 16)
                    hi(ws_hi[:, :], ws_raw[:, :]).then_inc(s_wsh, 1)
                if g == NG - 1:
                    act.wait_ge(s_setv, 18)
                    hi(tc_hi[:, :], HV[:, :]).then_inc(s_seta, 1)
            shared(0, 0)
            routed_slots(0)
            shared(0, 1)
            act.wait_ge(s_ainit, 1)
            attention()
            shared(1, 0)
            routed_slots(1)
            shared(1, 1)

        @block.vector
        def _(dve):
            def lo(o, full, h):
                return dve.tensor_tensor(o, full, f32(h), ALU.subtract)

            def xt_lo(c):
                for kb in range(KB):
                    dve.wait_ge(s_xh, 2 * c + kb + 1)
                    lo(xT_lo[:, kb, :], XT[kb][:, :], xT_hi[:, kb, :]).then_inc(s_xl, 1)

            def norm_stats(k, g, place):
                for t in range(GT):
                    ins = dve.bn_stats(stats[:, place, t, :], acc[:, bass.ds(g * GT + t, 1), :].squeeze(1))
                ins.then_inc(s_st, 1)
                wait_apart(dve, s_st, k + 1)
                for t in range(GT):
                    ins = dve.bn_aggr(mv[:, place, t, :], stats[:, place, t, :])
                ins.then_inc(s_mv, 1)

            def norm_apply(k, g, place, kept=None):
                dve.wait_ge(s_rs, k + 1)
                if kept is not None:
                    dve.wait_ge(s_xc[place], 16 * kept)
                for t in range(GT):
                    ts = bass.ds(g * GT + t, 1)
                    ins = dve.tensor_scalar(xg[:, place, t, :], acc[:, ts, :].squeeze(1),
                                            mv[:, place, t, 0:1], rstd[:, place, t:t + 1],
                                            ALU.subtract, ALU.mult)
                ins.then_inc(s_xn, 1)

            def copy_logits(g, count, bank=LG):
                dve.wait_ge(s_lg, count)
                dve.tensor_copy(tiles(lg, g), bank[:, 0:GT * E].rearrange("p (t e) -> p t e", t=GT)).then_inc(s_lgc, 1)

            steps = [0]

            def chained(ins):
                steps[0] += 1
                ins.then_inc(s_rt, 1)
                dve.wait_ge(s_rt, steps[0])

            def choose(L):
                def b3(ap):
                    return ap.unsqueeze(2).to_broadcast([P, NT, E])
                dve.wait_ge(s_lgc, (L + 1) * NG)
                dve.tensor_reduce(mx[:, :], lg[:, :, :], AX.X, ALU.max).then_inc(s_mx, 1)
                dve.wait_ge(s_mx, L + 1)
                chained(dve.tensor_tensor(eq[:, :, :], lg[:, :, :], b3(mx[:, :]), ALU.is_equal))
                chained(dve.tensor_tensor(eq[:, :, :], eq[:, :, :], pref[:, :, :].to_broadcast([P, NT, E]), ALU.mult))
                chained(dve.tensor_reduce(m2[:, :], eq[:, :, :], AX.X, ALU.max))
                dve.tensor_tensor(oh[:, :, :], eq[:, :, :], b3(m2[:, :]), ALU.is_equal).then_inc(s_oh, 1)

            def slot_tables(L):
                dve.wait_ge(s_pfc, L + 1)
                src, d, place = pfx[:, 1, :, :], 1, 0
                while d < NT:
                    dst = cum[:, place, :, :]
                    dve.tensor_copy(dst[:, 0:d, :], src[:, 0:d, :])
                    chained(dve.tensor_tensor(dst[:, d:NT, :], src[:, d:NT, :], src[:, 0:NT - d, :], ALU.add))
                    src, d, place = dst, 2 * d, 1 - place
                assert place == 1
                last = src[:, NT - 1:NT, :].rearrange("p a e -> p e a")
                chained(dve.tensor_tensor(cmp_t[:, :, :], last.to_broadcast([P, E, NT]),
                                       thr[:, :, :].to_broadcast([P, E, NT]), ALU.is_gt))
                chained(dve.tensor_reduce(ne[:, 3, :], cmp_t[:, :, :], AX.X, ALU.add))
                src, d, where = ne[:, 3, :], 1, 0
                while d < E:
                    dst = ne[:, where, :]
                    dve.tensor_copy(dst[:, 0:d], src[:, 0:d])
                    chained(dve.tensor_tensor(dst[:, d:E], src[:, d:E], src[:, 0:E - d], ALU.add))
                    src, d, where = dst, 2 * d, 1 - where
                before = ne[:, where, :]
                chained(dve.tensor_tensor(before, src, ne[:, 3, :], ALU.subtract))
                dve.tensor_scalar(ne[:, 2, :], before, float(P), None, ALU.mult).then_inc(s_cum, 1)
                dve.tensor_copy(after_e[:, :], src[0:1, :])
                chained(dve.tensor_tensor(se[:, :, :], sidx[:, :, :].to_broadcast([1, NS, E - 1]),
                                       src[0:1, 0:E - 1].unsqueeze(1).to_broadcast([1, NS, E - 1]), ALU.is_ge))
                chained(dve.tensor_reduce(sef[:, :], se[:, :, :], AX.X, ALU.add))
                dve.tensor_copy(slot_e[:, :], sef[:, :]).then_inc(s_tab, 1)

            def s_mult(L, g, fb):
                q = 4 * (L * NG + g) + fb
                dve.wait_ge(s_sg, q + 1)
                dve.wait_ge(s_u, q + 1)
                dve.tensor_tensor(hf[:, fb % 2, :], sg[:, fb % 2, :], U2[fb % 2][:, :],
                                  ALU.mult).then_inc(s_h, 1)

            def s_lo(L, g, fb):
                dve.wait_ge(s_hh, 4 * (L * NG + g) + fb + 1)
                lo(hT_lo[:, fb, :], hf[:, fb % 2, :], hT_hi[:, fb, :]).then_inc(s_hl, 1)

            def shared_group(L, g, following, scales={}):
                n = L * NG + g
                for fb in range(FB):
                    for row_group in scales.get(fb, ()):
                        scale_rows(L, row_group)
                    if fb >= 2:
                        dve.wait_ge(s_hl, 4 * n + fb - 1)
                    s_mult(L, g, fb)
                    if fb > 0:
                        s_lo(L, g, fb - 1)
                s_lo(L, g, FB - 1)
                if following is not None:
                    xt_lo(following)
                for row_group in scales.get(FB, ()):
                    scale_rows(L, row_group)
                if L == 1 and g >= NH:
                    wait_apart(dve, s_fin[g], 16 * GT)
                for a in range(2):
                    dve.wait_ge(s_d, 2 * n + a + 1)
                    half = acc[:, bass.ds(g * GT + 2 * a, 2), :]
                    dve.scalar_tensor_tensor(half, D2[a][:, :].rearrange("p (t h) -> p t h", t=2), 0.5, half,
                                             ALU.mult, ALU.add).then_inc(s_add, 1)

            def scale_rows(L, g):
                half = g % 2
                dve.wait_ge(s_rl[half], 16 * (L * NG // 2 + g // 2 + 1))
                for t in range(GT):
                    r = rows[:, half * GT + t, :]
                    ins = dve.tensor_scalar(r, r, score[:, bass.ds(g * GT + t, 1)], None, ALU.mult)
                ins.then_inc(s_scl, 1)

            def shared(L, half):
                if half == 0:
                    choose(L)
                xt_lo(c_s(L, half * NH))
                if half == 0:
                    slot_tables(L)
                    dve.wait_ge(s_sc, L + 1)
                for g in half_groups(half):
                    if L == 0 and g == NG - 2:
                        wait_apart(dve, s_ga[0], 64)
                        norm_stats(k_ln2(0), 0, 0)
                    if L == 0 and g == NG - 1:
                        norm_apply(k_ln2(0), 0, 0)
                        wait_apart(dve, s_ga[1], 64)
                        norm_stats(k_ln2(1), GB, 0)
                    shared_group(L, g, c_s(L, g + 1) if g % NH < NH - 1 else c_ln2(0) if L == 0 and half else None,
                                 scales=SCALED[g] if g < len(SCALED) else {})
                    if L == 0 and g == NH:
                        cut_w_io()

            SCALED = [{0: (0, 1), FB: (2,)}, {1: (3,), 3: (4,), FB: (5,)}, {1: (6,), 3: (7,)}]

            MXT, MU, MHT = B[0], B[3], B[4]

            def m_x_lo(L, s):
                dve.wait_ge(s_mxh, L * NS + s + 1)
                lo(xT_lo[:, :, 0:P], MXT[:, 0:KB * P].rearrange("p (k t) -> p k t", k=KB),
                   xT_hi[:, :, 0:P]).then_inc(s_mxl, 1)

            def routed_body(L, i, last=False):
                for j in range(RING):
                    s = i * RING + j
                    dve.wait_ge(s_msg, L * NS + s + 1)
                    dve.wait_ge(s_mu, L * NS + s + 1)
                    dve.tensor_tensor(hf[:, 0, :], sg[:, 0, :], MU[:, :], ALU.mult).then_inc(s_mh, 1)
                    if not (last and j == RING - 1):
                        m_x_lo(L, s + 1)
                    dve.wait_ge(s_mhh, L * NS + s + 1)
                    lo(hT_lo[:, :, 0:P], MHT[:, :].rearrange("p (f t) -> p f t", f=FB),
                       hT_hi[:, :, 0:P]).then_inc(s_mhl, 1)

            def routed_slots(L):
                m_x_lo(L, 0)
                with dve.Fori(0, NS // RING - 1) as i:
                    routed_body(L, i)
                routed_body(L, NS // RING - 1, last=True)

            def conv_start(n, b):
                if not isinstance(n, int) or n > 0:
                    dve.wait_ge(s_v, 4 * n)
                dve.tensor_copy(u[:, :, 0:3], halo[:, b, :, :]).then_inc(s_hal, 1)

            def tap(n, b, cb, k):
                q = 4 * n + cb
                vb = v[:, b, cb, :]
                if k == 2:
                    dve.wait_ge(s_hal, n + 1)
                    dve.wait_ge(s_tap3, q + 1)
                else:
                    dve.wait_ge(s_tap, 2 * q + 2 - k)
                dve.scalar_tensor_tensor(vb, u[:, cb, k:k + GN], vec[:, cb, k:k + 1], vb,
                                         ALU.mult, ALU.add).then_inc(s_tap if k else s_v, 1)

            def save_halo(b):
                dve.tensor_copy(halo[:, b, :, :], u[:, :, GN:GN + 3]).then_inc(s_halo, 1)

            def attn_group(n, b, prev=True, u_next=True, ln2_next=True):
                g = group_of(n, b, 0)
                for t in range(GT):
                    q = 4 * n + t
                    if t == 0 and u_next:
                        conv_start(n + 1, 1 - b)
                    dve.wait_ge(s_vh, q + 1)
                    lo(vT_lo[:, :], VT[:, :], vT_hi[:, :]).then_inc(s_vl, 1)
                    if t == 3:
                        if prev:
                            copy_logits(group_of(n, b, -1), NG + n)
                        add_out(n, g, 0)
                    if u_next:
                        tap(n + 1, 1 - b, t, 2)
                    if t == 1 and prev:
                        norm_stats(k_ln3(n - 1), group_of(n, b, -1), 1)
                    if t == 2 and ln2_next:
                        wait_apart(dve, s_ga[b], gathers_of(n, b, 2))
                        norm_stats(k_ln2(n + 2), group_of(n, b, 2), 0)
                    if t == 3 and ln2_next:
                        xt_lo(c_ln2(n + 2))
                    dve.wait_ge(s_z, q + 1)
                    for a in range(2):
                        zin = Z2[a][:, 0:2 * ZN].rearrange("p (c z) -> p c z", c=2)[:, :, P:ZN]
                        dve.tensor_copy(sf[:, 0, 2 * a:2 * a + 2, :], zin)
                        ins = dve.tensor_copy(sf[:, 1, 2 * a:2 * a + 2, :], zin)
                    ins.then_inc(s_zs, 1)
                    if u_next:
                        tap(n + 1, 1 - b, t, 1)
                        tap(n + 1, 1 - b, t, 0)
                        if t == GT - 1:
                            save_halo(1 - b)
                    if t == 1 and prev:
                        norm_apply(k_ln3(n - 1), group_of(n, b, -1), 1, NG // 2 + n - 1)
                    if t == 2 and ln2_next:
                        norm_apply(k_ln2(n + 2), group_of(n, b, 2), 0)
                    dve.wait_ge(s_sh, q + 1)
                    lo(HH[HB:2 * HB, b, :], SB_[HB:2 * HB, 0:P], HH[HB:2 * HB, b, :]).then_inc(s_sl, 1)
                    if t == 0 and prev:
                        add_out(n - 1, group_of(n, b, -1), 1)
                        wait_apart(dve, s_x2, 2 * n)

            def attention():
                conv_start(0, 0)
                for cb in range(CB):
                    for k in (2, 1, 0):
                        tap(0, 0, cb, k)
                    if cb == 0:
                        norm_apply(k_ln2(1), GB, 0)
                save_halo(0)
                xt_lo(c_ln2(1))
                attn_group(0, 0, prev=False)
                attn_group(1, 1)
                with dve.Fori(1, GB - 1) as i:
                    for b in range(NB):
                        where[0] = i
                        attn_group(NB * i + b, b)
                where[0] = None
                attn_group(NG - 2, 0, ln2_next=False)
                attn_group(NG - 1, 1, u_next=False, ln2_next=False)
                last = (NB - 1) * GB + GB - 1
                add_out(NG - 1, last, 1)
                wait_apart(dve, s_x2, 2 * NG)
                norm_stats(k_ln3(NG - 1), last, 1)
                norm_apply(k_ln3(NG - 1), last, 1, NG // 2 + NG - 1)
                copy_logits(last, 2 * NG)

            where = [None]

            def group_of(n, b, d):
                i = where[0] if where[0] is not None else (n - b) // 2
                b2 = (b + d) % 2
                return b2 * GB + i + (b + d - b2) // 2

            def gathers_of(n, b, d):
                i = where[0] if where[0] is not None else (n - b) // 2
                return 64 * (i + (1 + d // 2))

            def add_out(n, g, a):
                dve.wait_ge(s_o, 4 * n + 2 * a + 2)
                half = acc[:, bass.ds(g * GT + 2 * a, 2), :]
                dve.tensor_tensor(half, half, OB[:, :].rearrange("p (t h) -> p t h", t=2),
                                  ALU.add).then_inc(s_x2, 1)

            def cut_w_io():
                dve.wait_ge(s_wioh, 1)
                dve.tensor_tensor(win_lo[:, :, :].rearrange("p k c -> p (k c)"), wio_raw[:, 0, :],
                                  f32(win_hi[:, :, :].rearrange("p k c -> p (k c)")), ALU.subtract).then_inc(s_wiol, 1)
                dve.wait_ge(s_wioh, 2)
                dve.tensor_tensor(wout_lo[:, :, :].rearrange("p k c -> p (k c)"), wio_raw[:, 1, :],
                                  f32(wout_hi[:, :, :].rearrange("p k c -> p (k c)")), ALU.subtract).then_inc(s_wiol, 1)
                dve.memset(halo[:, :, :, :], 0.0)
                dve.memset(f32(HH[:, :, :]), 0.0).then_inc(s_ainit, 1)
                dve.wait_ge(s_ainit, 1)

            dve.wait_ge(s_small, 16 * 6)
            dve.tensor_copy(VO[:, 0, 0:1], bc[:, 0:1]).then_inc(s_setv, 1)
            dve.tensor_copy(VO[:, 1, 0:1], bc[:, 1:2]).then_inc(s_setv, 1)
            dve.memset(kpad[:, :], 0.0).then_inc(s_setv, 1)
            m, step = 1, 0
            while m < P:
                dve.wait_ge(s_setp, step + 1)
                dve.tensor_copy(VO[:, :, m:2 * m],
                                B[7][0:N, 0:2 * P].rearrange("n (a m) -> n a m", a=2)[:, :, 0:m])
                dve.tensor_copy(PQ[:, (step + 1) % 2, :, :],
                                B[7][0:N, 256:256 + 2 * N].rearrange("n (a m) -> n a m", a=2)).then_inc(s_setv, 1)
                m, step = 2 * m, step + 1
            assert (m, step) == (P, 7)

            def setup_response():
                dve.wait_ge(s_setp, 9)
                dve.tensor_copy(kpad[:, P - 1:2 * P - 1], B[6][0:1, 0:P]).then_inc(s_setv, 1)
                dve.wait_ge(s_setv, 11)
                dve.tensor_tensor(kpad[:, P - 1:P], kpad[:, P - 1:P], dd[:, :], ALU.add).then_inc(s_setv, 1)
                dve.tensor_copy(OQ[:, 0:P], B[6][0:N, P:2 * P])
                dve.tensor_copy(OQ[:, P:ZN], PQ[:, 1, 1, :]).then_inc(s_setv, 1)
                dve.tensor_copy(HV[:, P:ZN], B[5][:, 0:N]).then_inc(s_setv, 1)

            def setup_toeplitz():
                dve.wait_ge(s_setp, 10)
                dve.tensor_copy(HV[:, :], B[5][:, 0:ZN]).then_inc(s_setv, 1)

            def setup_toeplitz_lo():
                dve.wait_ge(s_seta, 3)
                dve.tensor_tensor(tc_lo[:, :], HV[:, :], f32(tc_hi[:, :]), ALU.subtract).then_inc(s_setv, 1)

            def setup_rows():
                dve.wait_ge(s_seta, 2)
                dve.tensor_tensor(rr_lo[0:HB, :, :, :].rearrange("p a b z -> p (a b z)"),
                                  rf[0:HB, :, :, :].rearrange("p a b z -> p (a b z)"),
                                  f32(rr_hi[0:HB, :, :, :].rearrange("p a b z -> p (a b z)")), ALU.subtract)
                dve.tensor_copy(bo_hl[0:1, :], bo_f[:, :]).then_inc(s_setv, 1)
                dve.wait_ge(s_setv, 15)
                dve.tensor_tensor(bo_t[:, :], bo_f[:, :], f32(bo_hl[0:1, :]), ALU.subtract).then_inc(s_setv, 1)
                dve.wait_ge(s_setv, 16)
                dve.tensor_copy(bo_hl[32:33, :], bo_t[:, :]).then_inc(s_setv, 1)

            dve.wait_ge(s_x[0], 16)
            norm_stats(k_r1(0), 0, 0)
            for g in range(NG):
                if g + 1 < NG:
                    dve.wait_ge(s_x[g + 1], 16)
                    norm_stats(k_r1(g + 1), g + 1, (g + 1) % 2)
                if g > 1:
                    dve.wait_ge(s_xt, 2 * (g - 1))
                norm_apply(k_r1(g), g, g % 2, g // 2 if g >= 2 else None)
                if g > 1:
                    copy_logits(g - 2, g - 1, LG1)
                if g == 2:
                    setup_response()
                if g == 5:
                    setup_rows()
                if g == 6:
                    dve.wait_ge(s_wsh, 1)
                    dve.tensor_tensor(ws_lo[:, :], ws_raw[:, :], f32(ws_hi[:, :]), ALU.subtract).then_inc(s_wsl, 1)
                if g == 7:
                    setup_toeplitz()
            for g in (NG - 2, NG - 1):
                copy_logits(g, g + 1, LG1)
            setup_toeplitz_lo()
            shared(0, 0)
            routed_slots(0)
            shared(0, 1)
            attention()
            shared(1, 0)
            routed_slots(1)
            shared(1, 1)

        @block.gpsimd
        def _(pool):
            done = [0]

            def row_step(ins):
                done[0] += 1
                ins.then_inc(s_row, 1)
                pool.wait_ge(s_row, done[0])

            def rsqrt(k, place):
                wait_apart(pool, s_mv, k + 1)
                pool.tensor_scalar(ve[:, place, :], mv[:, place, :, 1:2].squeeze(2), LN_EPS, None,
                                   ALU.add).then_inc(s_ve, 1)
                pool.wait_ge(s_ve, k + 1)
                pool.tensor_tensor(rstd[:, place, :], ve[:, place, :], mhalf[:, :], ALU.pow).then_inc(s_rs, 1)

            def token_rows(L):
                pool.wait_ge(s_cum, L + 1)
                t3 = pfx[:, 0, :, :]
                row_step(pool.tensor_tensor(t3, t3, cum[:, 0, :, :], ALU.add))
                row_step(pool.tensor_tensor(t3, t3, pfx[:, 1, :, :], ALU.subtract))
                row_step(pool.tensor_tensor(t3, t3, ne[:, 2:3, :].to_broadcast([P, NT, E]), ALU.add))
                row_step(pool.tensor_tensor(t3, t3, oh[:, :, :], ALU.mult))
                d = E // 2
                while d >= 1:
                    row_step(pool.tensor_tensor(t3[:, :, 0:d], t3[:, :, 0:d], t3[:, :, d:2 * d], ALU.add))
                    d //= 2
                row_step(pool.tensor_copy(pos[:, :], t3[:, :, 0:1].squeeze(2)))

            def scatter(L):
                for g in range(NG):
                    half, n = g % 2, L * NG + g
                    pool.wait_ge(s_scl, n + 1)
                    for t in range(GT):
                        tt = g * GT + t
                        pool.indirect_dma_start(
                            out=xs_dram, out_offset=bass.IndirectOffsetOnAxis(ap=pos[:, tt:tt + 1], axis=0),
                            in_=rows[:, half * GT + t, :], in_offset=None).then_inc(s_sct[half], 16)
                    if g in (1, 3, 5):
                        cut_part(L, g // 2)
                    if g == 5:
                        load_expert(L, 1)

            def load_expert(L, e, free=None):
                k = L * E + e
                if k > 0:
                    pool.wait_ge(s_wl, k)
                pool.dma_start(wr_raw[:, :], w_routed[e, :, :]).then_inc(s_wraw, 16)
                if free is not None:
                    wait_apart(pool, s_slot, free)
                pool.dma_start(wr_hi[:, e % 2, :], w_routed[e, :, :]).then_inc(s_wh, 16)

            def cut_part(L, i):
                if i == 0:
                    pool.wait_ge(s_wraw, 16 * (L * E + 1))
                    pool.wait_ge(s_wh, 16 * (L * E + 1))
                ws = slice(i * W // 3, (i + 1) * W // 3)
                ins = pool.tensor_tensor(wr_lo[:, 0, ws], wr_raw[:, ws], f32(wr_hi[:, 0, ws]), ALU.subtract)
                if i == 2:
                    ins.then_inc(s_wl, 1)

            def cut_expert(L, e):
                k = L * E + e
                pool.wait_ge(s_wraw, 16 * (k + 1))
                pool.wait_ge(s_wh, 16 * (k + 1))
                pool.tensor_tensor(wr_lo[:, e % 2, :], wr_raw[:, :], f32(wr_hi[:, e % 2, :]),
                                   ALU.subtract).then_inc(s_wl, 1)

            def route_rows(L):
                load_expert(L, 0)
                token_rows(L)
                scatter(L)
                cut_expert(L, 1)

            def experts(L):
                pool.wait_ge(s_tab, L + 1)
                for e in range(2, E):
                    end = pool.value_load(after_e[0:1, e - 2:e - 1], min_val=0, max_val=NS)
                    load_expert(L, e, end + (L * NS + 1))
                    cut_expert(L, e)

            def gather(g, s):
                for t in range(GT):
                    gather_tile(g, t, s)

            def gather_tile(g, t, s):
                tt = g * GT + t
                pool.indirect_dma_start(
                    out=acc[:, tt, :], out_offset=None, in_=ys_dram,
                    in_offset=bass.IndirectOffsetOnAxis(ap=pos[:, tt:tt + 1], axis=0),
                    compute_op=ALU.add).then_inc(s, 16)

            def y_all_stored(L):
                for j in range(RING):
                    pool.wait_ge(s_yst[j], 16 * (NS // RING) * (L + 1))

            def pstep(ins, n):
                ins.then_inc(s_const, 1)
                pool.wait_ge(s_const, n)

            pool.memset(mhalf[:, :], -0.5)
            pool.memset(anti[:, :], 0.0)
            pstep(pool.memset(ident[:, :], 0.0), 1)
            pstep(pool.affine_select(ident[:, :], ident[:, :], pattern=[[-1, P]], compare_op=ALU.not_equal,
                                     fill=1.0, base=0, channel_multiplier=1), 2)
            pstep(pool.affine_select(anti[:, :], anti[:, :], pattern=[[1, P]], compare_op=ALU.not_equal,
                                     fill=1.0, base=-(P - 1), channel_multiplier=1), 3)
            pool.memset(f32(ones_r[:, :]), 1.0)
            pool.memset(f32(rr_lo[:, :, :, :]), 0.0)
            pool.memset(rf[:, :, :, :], 0.0)
            pool.memset(f32(bo_hl[:, :]), 0.0)
            pool.memset(ones[:, :], 1.0)
            pstep(pool.memset(upper[:, :], 0.0), 4)
            pstep(pool.affine_select(upper[:, :], upper[:, :], pattern=[[-1, P]], compare_op=ALU.is_ge,
                                     fill=1.0, base=0, channel_multiplier=1), 5)
            pstep(pool.iota(pref[:, :, :].rearrange("p a e -> p (a e)"), pattern=[[-1, E]], base=E,
                            channel_multiplier=0, allow_small_or_imprecise_dtypes=True), 6)
            pstep(pool.iota(thr[:, :, :].rearrange("p a e -> p (a e)"), pattern=[[P, NT]], base=0,
                            channel_multiplier=0, allow_small_or_imprecise_dtypes=True), 7)
            pstep(pool.memset(thr[:, :, 0:1], -1.0), 8)
            pstep(pool.iota(sidx[:, :, :].rearrange("p a e -> p (a e)"), pattern=[[1, NS]], base=0,
                            channel_multiplier=0, allow_small_or_imprecise_dtypes=True), 9)
            pool.memset(rows[:, :, :], 0.0).then_inc(s_const, 1)
            pool.wait_ge(s_const, 10)
            for g in range(NG):
                rsqrt(k_r1(g), g % 2)
                if g == NG // 2 - 1:
                    s0 = 0
                    while s0 < NS:
                        c = min(2 * GT, NS - s0)
                        pool.dma_start(xs_slot[:, s0:s0 + c, :], rows[:, 0:c, :]).then_inc(s_zero, 16)
                        s0 += c
            pool.wait_ge(s_zero, 16 * ZERO_STORES)
            pool.wait_ge(s_setv, 19)
            route_rows(0)
            experts(0)
            pool.wait_ge(s_wl, E)
            pool.dma_start(wio_raw[:, 0, :], w_in.rearrange("p k c -> p (k c)")).then_inc(s_wio, 16)
            pool.dma_start(wio_raw[:, 1, :], w_out.rearrange("p k c -> p (k c)")).then_inc(s_wio, 16)
            y_all_stored(0)
            gather(0, s_ga[0])
            pool.wait_ge(s_add, 2 * (GB + 1))
            gather(GB, s_ga[1])
            for n in range(2):
                rsqrt(k_ln2(n), 0)
            gather(1, s_ga[0])
            for n in range(NG):
                b, i = n % 2, n // 2
                for t in range(GT):
                    if t == 1 and n > 0:
                        rsqrt(k_ln3(n - 1), 1)
                    if t == 2 and n + 2 < NG:
                        rsqrt(k_ln2(n + 2), 0)
                    q = 4 * n + t
                    pool.wait_ge(s_yh, q + 1)
                    pool.tensor_tensor(y_lo[:, t % 2, :, :], yf[:, t % 2, :, :],
                                       f32(y_hi[:, t % 2, :, :]), ALU.subtract).then_inc(s_yl, 1)
                    if n + 3 < NG:
                        gather_tile((1 - b) * GB + (n + 3) // 2, t, s_ga[1 - b])
            rsqrt(k_ln3(NG - 1), 1)
            route_rows(1)
            experts(1)
            y_all_stored(1)
            for g in (*half_groups(1), *half_groups(0)):
                gather(g, s_fin[g])

        @block.sync
        def _(sp):
            sp.dma_start(A2[:, :], ssm_a).then_inc(s_small, 16)
            sp.dma_start(bc[:, :], ssm_bc).then_inc(s_small, 16)
            sp.dma_start(dd[:, :], ssm_d).then_inc(s_small, 16)
            sp.dma_start(gw_f[:, :, :], gate_w).then_inc(s_small, 16)
            sp.dma_start(vec[:, :, :], vecs).then_inc(s_small, 16)
            sp.dma_start(bo_f[:, :], b_out).then_inc(s_small, 16)
            for g in range(NG):
                sp.dma_start(tiles(acc, g), tiles(xt, g)).then_inc(s_x[g], 16)
                if g == NG // 2:
                    sp.dma_start(ws_raw[:, :], w_shared).then_inc(s_wsraw, 16)

            def slot_load(L, s, j):
                sp.dma_start(rows[:, j, :], xs_slot[:, bass.ds(s, 1), :].squeeze(1)).then_inc(s_xsl[j], 16)

            def slot_store(L, s, j):
                sp.wait_ge(s_ye, L * NS + s + 1)
                sp.dma_start(ys_slot[:, bass.ds(s, 1), :].squeeze(1), rows[:, GT + j, :]).then_inc(s_yst[j], 16)

            def routed_slots(L):
                for a in range(2):
                    sp.wait_ge(s_sct[a], 64 * (NG // 2) * (L + 1))
                for j in range(RING):
                    slot_load(L, j, j)
                with sp.Fori(0, NS // RING - 1) as i:
                    for j in range(RING):
                        s = i * RING + j
                        sp.wait_ge(s_mt, L * NS + s + 1)
                        slot_load(L, s + RING, j)
                        slot_store(L, s, j)
                for j in range(RING):
                    slot_store(L, NS - RING + j, j)

            def keep(k, place, g):
                sp.wait_ge(s_xn, k + 1)
                sp.dma_start(tiles(xn, g), xg[:, place, :, :]).then_inc(s_xc[place], 16)

            def first_shared_load(L):
                if L == 0:
                    sp.wait_ge(s_xc[0], 16 * (NG // 2))
                    sp.wait_ge(s_xt, 2 * (t_r1(NG - 2) + 1))
                else:
                    sp.wait_ge(s_xc[1], 16 * (NG // 2 + L * NG - 1))
                    sp.wait_ge(s_xt, 2 * (t_ln2(NG - 1) + 1))
                sp.dma_start(xg[:, 0, :, :], tiles(xn, 0)).then_inc(s_xg[0], 16)

            def first_loads(L):
                sp.wait_ge(s_xc[1], 16 * (NG // 2 + L * NG))
                shared_loads(L, (1,))
                for g in range(2):
                    load_rows(L, g)
                shared_loads(L, range(2, NH))
                for g in range(2, NG):
                    load_rows(L, g)
                shared_loads(L, range(NH, NH + 2))

            def load_rows(L, g):
                n = L * NG + g
                if n == 0:
                    sp.wait_ge(s_zero, 16 * ZERO_STORES)
                if n >= 2:
                    sp.wait_ge(s_sct[g % 2], 64 * (n // 2))
                sp.dma_start(rows[:, g % 2 * GT:(g % 2 + 1) * GT, :], tiles(xn, g)).then_inc(s_rl[g % 2], 16)

            def shared_loads(L, groups):
                for g in groups:
                    sp.wait_ge(s_xt, 2 * (t_s(L, g) - 1))
                    sp.dma_start(xg[:, g % 2, :, :], tiles(xn, g)).then_inc(s_xg[g % 2], 16)

            for g in range(NG):
                if g == NG - 1:
                    first_shared_load(0)
                keep(k_r1(g), g % 2, g)
                if g == 1:
                    sp.wait_ge(s_setv, 13)
                    sp.dma_start(k_dram.ap(), kpad[:, :]).then_inc(s_kst, 16)
                    sp.dma_start(oq_dram, OQ[:, :]).then_inc(s_oqst, 16)
                if g == 2:
                    sp.wait_ge(s_kst, 16)
                    hankel = bass.AP(k_dram, 0, [[1, P], [1, P]])
                    sp.dma_start(HV[:, 0:P], hankel).then_inc(s_hank, 16)
                    sp.wait_ge(s_oqst, 16)
                    sp.wait_ge(s_const, 7)
                    for half in range(2):
                        for cb in range(CB):
                            r0 = half * HB + cb * N
                            sp.dma_start(rf[r0:r0 + N, cb // 2, cb % 2, :], oq_dram).then_inc(s_rf, 16)
            first_loads(0)
            routed_slots(0)
            shared_loads(0, range(NH + 2, NG))
            with sp.Fori(0, GB - 1) as i:
                for b in range(NB):
                    keep(k_ln3(NB * i + b), 1, b * GB + i)
            for b in range(NB):
                if b == NB - 1:
                    first_shared_load(1)
                keep(k_ln3(NG - NB + b), 1, b * GB + GB - 1)
            first_loads(1)
            routed_slots(1)
            shared_loads(1, range(NH + 2, NG))
            for g in range(NG):
                sp.wait_ge(s_fin[g], 16 * GT)
                if g >= NH:
                    sp.wait_ge(s_add, 2 * (NG + g + 1))
                sp.dma_start(tiles(ot, g), tiles(acc, g)).then_inc(s_out, 16)
            sp.wait_ge(s_out, 16 * NG)


def kernel(L0_attn_x, L0_attn_W_in, L0_attn_b_in, L0_attn_conv_w, L0_attn_conv_b, L0_attn_A, L0_attn_Bp,
           L0_attn_Cp, L0_attn_Dp, L0_attn_W_out, L0_attn_b_out, L0_ffn_gate_w, L0_ffn_shared_gate,
           L0_ffn_shared_up, L0_ffn_shared_down, L0_ffn_r_gate, L0_ffn_r_up, L0_ffn_r_down):
    import numpy as np
    import concourse.bacc as bacc
    from concourse.bass_utils import run_bass_kernel_spmd

    x = np.asarray(L0_attn_x)
    nb, s, h = x.shape

    def blocks(w):
        return np.ascontiguousarray(w.reshape(-1, P, w.shape[-1]).transpose(1, 0, 2))

    def expert(g, u, d):
        return np.concatenate([blocks(np.asarray(w).T).reshape(P, -1) for w in (g, u, d)], axis=1)

    r_g, r_u, r_d = (np.asarray(w) for w in (L0_ffn_r_gate, L0_ffn_r_up, L0_ffn_r_down))
    A = np.asarray(L0_attn_A)
    cw = np.asarray(L0_attn_conv_w)[:, 0, :]
    per_channel = np.concatenate([cw, np.asarray(L0_attn_conv_b)[:, None], np.asarray(L0_attn_b_in)[:, None]], axis=1)
    arrays = {
        "x": x.reshape(nb * s, h),
        "w_routed": np.stack([expert(r_g[e], r_u[e], r_d[e]) for e in range(r_g.shape[0])]),
        "w_shared": expert(L0_ffn_shared_gate, L0_ffn_shared_up, L0_ffn_shared_down),
        "gate_w": blocks(np.asarray(L0_ffn_gate_w).T),
        "w_in": blocks(np.asarray(L0_attn_W_in)),
        "w_out": blocks(np.asarray(L0_attn_W_out)),
        "vecs": blocks(per_channel),
        "b_out": np.asarray(L0_attn_b_out)[None, :],
        "ssm_a": np.concatenate([A, A.T], axis=1),
        "ssm_bc": np.stack([np.asarray(L0_attn_Bp), np.asarray(L0_attn_Cp)], axis=1),
        "ssm_d": np.asarray(L0_attn_Dp)[None, :],
    }
    arrays = {k: np.ascontiguousarray(a) for k, a in arrays.items()}
    nc = bacc.Bacc("TRN2", target_bir_lowering=False, num_devices=1)
    aps = {k: nc.dram_tensor(k, a.shape, mybir.dt.from_np(a.dtype), kind="ExternalInput").ap()
           for k, a in arrays.items()}
    out = nc.dram_tensor("out", (nb * s, h), F32, kind="ExternalOutput").ap()
    build(nc, *aps.values(), out)
    r = run_bass_kernel_spmd(nc, [arrays], core_ids=[0])
    return r.results[0]["out"].reshape(nb, s, h)
```
